# Optimizing a Trainium2 kernel written in Bass

```python
import numpy as np
import jax
import jax.numpy as jnp

def _softmax(x, axis=-1):
    return jax.nn.softmax(x, axis=axis)

def _gelu(x):
    return jax.nn.gelu(x, approximate=True)

def _silu(x):
    return jax.nn.silu(x)

def _sigmoid(x):
    return jax.nn.sigmoid(x)

def _layernorm(x, axis=-1, eps=1e-05):
    m = jnp.mean(x, axis=axis, keepdims=True)
    v = jnp.var(x, axis=axis, keepdims=True)
    return (x - m) / jnp.sqrt(v + eps)

def _scatter_add(tgt, idx, src, axis=0):
    return tgt.at[idx].add(src)

def _segment_sum(src, seg, n):
    return jax.ops.segment_sum(src, seg, n)
kernel_name = 'mk_cond_seq_d1_seqx_r2_71ef8e'

def setup_inputs(seed: int=0):
    np.random.seed(seed)
    _w = jnp.asarray

    def _rec_inputs():
        import jax
        import jax.numpy as jnp
        _rk = jax.random.key(seed)
        x = -9.26e-05 + 0.9999 * jax.random.normal(jax.random.fold_in(_rk, 1), (8, 1024, 576), jnp.float32)
        _lenS = 1024 - jax.random.randint(jax.random.fold_in(_rk, 7), (8,), 0, max(1, 1024 // 4) + 1, jnp.int32)
        _lenS2 = 1024 - jax.random.randint(jax.random.fold_in(_rk, 8), (8,), 0, max(1, 1024 // 4) + 1, jnp.int32)
        cond_1152 = 0.00338249 + 1.00093 * jax.random.normal(jax.random.fold_in(_rk, 11), (8, 576), jnp.float32)
        return (x, cond_1152)
    x, cond_1152 = _rec_inputs()

    def _L0_cond_setup():
        import jax, jax.numpy as jnp
        import numpy as np
        N, T, D, H = (32, 512, 576, 16)
        DH = D // H
        MLP = int(D * 4.0)
        EPS = 1e-06

        def _layernorm(x):
            m = jnp.mean(x, axis=-1, keepdims=True)
            v = jnp.var(x, axis=-1, keepdims=True)
            return (x - m) * jax.lax.rsqrt(v + EPS)

        def _modulate(x, shift, scale):
            return x * (1.0 + scale[:, None, :]) + shift[:, None, :]

        def _attention(x, qkv_w, qkv_b, proj_w, proj_b):
            n, t, d = x.shape
            scale = DH ** (-0.5)
            qkv = x @ qkv_w + qkv_b
            qkv = qkv.reshape(n, t, 3, H, DH)
            q, k, v = (qkv[:, :, 0], qkv[:, :, 1], qkv[:, :, 2])
            attn = jnp.einsum('nthd,ntkd->nthk', q * scale, k)
            attn = jax.nn.softmax(attn, axis=-1)
            out = jnp.einsum('nthk,ntkd->nthd', attn, v)
            out = out.transpose(0, 2, 1, 3).reshape(n, t, d)
            return out @ proj_w + proj_b

        def _mlp(x, fc1_w, fc1_b, fc2_w, fc2_b):
            h = jax.nn.gelu(x @ fc1_w + fc1_b, approximate=False)
            return h @ fc2_w + fc2_b
        key = jax.random.key(seed)
        ks = jax.random.split(key, 14)
        s = 0.02
        return {'x': jax.random.normal(ks[0], (N, T, D), jnp.float32), 'c': jax.random.normal(ks[1], (N, D), jnp.float32), 'qkv_w': jax.random.normal(ks[2], (D, 3 * D), jnp.float32) * s, 'qkv_b': jax.random.normal(ks[3], (3 * D,), jnp.float32) * s, 'proj_w': jax.random.normal(ks[4], (D, D), jnp.float32) * s, 'proj_b': jax.random.normal(ks[5], (D,), jnp.float32) * s, 'fc1_w': jax.random.normal(ks[6], (D, MLP), jnp.float32) * s, 'fc1_b': jax.random.normal(ks[7], (MLP,), jnp.float32) * s, 'fc2_w': jax.random.normal(ks[8], (MLP, D), jnp.float32) * s, 'fc2_b': jax.random.normal(ks[9], (D,), jnp.float32) * s, 'ada_w': jax.random.normal(ks[10], (D, 6 * D), jnp.float32) * s, 'ada_b': jax.random.normal(ks[11], (6 * D,), jnp.float32) * s}
    _L0_cond_all = _L0_cond_setup()
    _L0_cond_in = {k: v for k, v in _L0_cond_all.items() if k in ('qkv_w', 'qkv_b', 'proj_w', 'proj_b', 'fc1_w', 'fc1_b', 'fc2_w', 'fc2_b', 'ada_w', 'ada_b')}
    del _L0_cond_all
    return {'x': x, 'cond_1152': cond_1152, 'L0_cond_qkv_w': _L0_cond_in['qkv_w'], 'L0_cond_qkv_b': _L0_cond_in['qkv_b'], 'L0_cond_proj_w': _L0_cond_in['proj_w'], 'L0_cond_proj_b': _L0_cond_in['proj_b'], 'L0_cond_fc1_w': _L0_cond_in['fc1_w'], 'L0_cond_fc1_b': _L0_cond_in['fc1_b'], 'L0_cond_fc2_w': _L0_cond_in['fc2_w'], 'L0_cond_fc2_b': _L0_cond_in['fc2_b'], 'L0_cond_ada_w': _L0_cond_in['ada_w'], 'L0_cond_ada_b': _L0_cond_in['ada_b']}

def reference(x, cond_1152, L0_cond_qkv_w, L0_cond_qkv_b, L0_cond_proj_w, L0_cond_proj_b, L0_cond_fc1_w, L0_cond_fc1_b, L0_cond_fc2_w, L0_cond_fc2_b, L0_cond_ada_w, L0_cond_ada_b):
    import jax
    import jax.numpy as jnp

    def _L0_cond_ref(x, c, qkv_w, qkv_b, proj_w, proj_b, fc1_w, fc1_b, fc2_w, fc2_b, ada_w, ada_b):
        import jax, jax.numpy as jnp
        import numpy as np
        N, T, D, H = (32, 512, 576, 16)
        DH = D // H
        MLP = int(D * 4.0)
        EPS = 1e-06

        def _layernorm(x):
            m = jnp.mean(x, axis=-1, keepdims=True)
            v = jnp.var(x, axis=-1, keepdims=True)
            return (x - m) * jax.lax.rsqrt(v + EPS)

        def _modulate(x, shift, scale):
            return x * (1.0 + scale[:, None, :]) + shift[:, None, :]

        def _attention(x, qkv_w, qkv_b, proj_w, proj_b):
            n, t, d = x.shape
            scale = DH ** (-0.5)
            qkv = x @ qkv_w + qkv_b
            qkv = qkv.reshape(n, t, 3, H, DH)
            q, k, v = (qkv[:, :, 0], qkv[:, :, 1], qkv[:, :, 2])
            attn = jnp.einsum('nthd,ntkd->nthk', q * scale, k)
            attn = jax.nn.softmax(attn, axis=-1)
            out = jnp.einsum('nthk,ntkd->nthd', attn, v)
            out = out.transpose(0, 2, 1, 3).reshape(n, t, d)
            return out @ proj_w + proj_b

        def _mlp(x, fc1_w, fc1_b, fc2_w, fc2_b):
            h = jax.nn.gelu(x @ fc1_w + fc1_b, approximate=False)
            return h @ fc2_w + fc2_b
        ada = jax.nn.silu(c) @ ada_w + ada_b
        shift_msa, scale_msa, gate_msa, shift_mlp, scale_mlp, gate_mlp = jnp.split(ada, 6, axis=1)
        x = x + gate_msa[:, None, :] * _attention(_modulate(_layernorm(x), shift_msa, scale_msa), qkv_w, qkv_b, proj_w, proj_b)
        x = x + gate_mlp[:, None, :] * _mlp(_modulate(_layernorm(x), shift_mlp, scale_mlp), fc1_w, fc1_b, fc2_w, fc2_b)
        return x
    x = _L0_cond_ref(x, cond_1152, L0_cond_qkv_w, L0_cond_qkv_b, L0_cond_proj_w, L0_cond_proj_b, L0_cond_fc1_w, L0_cond_fc1_b, L0_cond_fc2_w, L0_cond_fc2_b, L0_cond_ada_w, L0_cond_ada_b)
    return x

_drawn_inputs = setup_inputs


def setup_inputs(seed=0):
    import zlib

    import numpy as np

    out = dict(_drawn_inputs(seed))
    spreads = {}
    factors = {'L0_cond_qkv_w': 3.089,
     'L0_cond_qkv_b': 8.0,
     'L0_cond_proj_w': 3.082,
     'L0_cond_proj_b': 8.0,
     'L0_cond_fc1_b': 8.0,
     'L0_cond_fc2_b': 8.0,
     'L0_cond_ada_b': 8.0}
    for name, (base, spread) in spreads.items():
        noise = np.random.default_rng([zlib.crc32(name.encode()), seed]).standard_normal(out[name].shape)
        drawn = base * np.exp(spread * noise) if base else spread * noise
        out[name] = jnp.asarray(drawn.astype(out[name].dtype))
    for name, factor in factors.items():
        out[name] = (out[name] * factor).astype(out[name].dtype)
    return out
```

```python
from contextlib import ExitStack

import concourse.bass as bass
from concourse import mybir

F32 = mybir.dt.float32
F16 = mybir.dt.float16
BF16 = mybir.dt.bfloat16
ALU = mybir.AluOpType
ACT = mybir.ActivationFunctionType
AX = mybir.AxisListType

P = 128
HEADS = 16
EPS = 1e-6
WSCALE = 256.0
OFF = -1e30
RING = 8
LAGS = 3
VECTORS = 6
SHIFT_MSA, SCALE_MSA, GATE_MSA, SHIFT_MLP, SCALE_MLP, GATE_MLP = range(VECTORS)
STAGES = 6
IDENT_SET, BIAS_SET, CONSTANTS_SET = 2, 3, 17


def block_kernel(nc, x, cond, qkv_w, qkv_b, proj_w, proj_b, fc1_w, fc1_b, fc2_w, fc2_b, ada_w, ada_b, out):
    B, T, D = x.shape
    DH = D // HEADS
    MLP = fc1_w.shape[1]
    NT = T // P
    NG = NT // 4
    KC = -(-D // P)
    KF = D // P
    REM = D - KF * P
    MF = MLP // P
    HALF = D // 2
    MB = 256
    NB = T // MB
    SCALE = DH ** -0.5
    E = P // HEADS
    NBLK = T // E
    GROUPS = NBLK // 4
    HC = 3 * DH
    QC = 3 * D // 4
    SPLITS = NG * KC * 3
    S_LN1, S_ATT, S_LN2 = 0, NG * KC, 2 * NG * KC
    assert REM == 64 and MF % 3 == 0 and SPLITS % 2 == 0 and NBLK == P and E == NT and GROUPS % RING == 0

    with ExitStack() as ctx:
        def sb(name, shape, dt):
            return ctx.enter_context(nc.sbuf_tensor(name, shape, dt))

        def sem(name):
            return ctx.enter_context(nc.semaphore(name))

        qkv_dram = nc.dram_tensor("qkv", (T, 3 * D), F32).ap()
        mod_dram = nc.dram_tensor("modulation", (B, VECTORS, KC * P), F32).ap()

        wq_h, wq_l = sb("wq_h", [P, KC, 3 * D], F16), sb("wq_l", [P, KC, 3 * D], F16)
        wp_h, wp_l = sb("wp_h", [P, KC, D], F16), sb("wp_l", [P, KC, D], F16)
        w1_h, w1_l = sb("w1_h", [P, KC, MLP], F16), sb("w1_l", [P, KC, MLP], F16)
        w2_h, w2_l = sb("w2_h", [P, MF, D], F16), sb("w2_l", [P, MF, D], F16)

        tok = sb("tok", [P, NT, D], F32)
        xr = sb("xr", [P, (2 * KC - 1) * T], F16)
        xh = xr[:, 0:KC * T].rearrange("p (c t) -> p c t", c=KC)
        xl = xr[:, KC * T:].rearrange("p (c t) -> p c t", c=KC - 1)
        att = xr[:, 0:8192].bitcast(F32).rearrange("p (k s t) -> p k s t", k=4, s=2)
        q_t, k_t, probs, probs_t = (att[:, k] for k in range(4))
        vr = sb("vr", [P, 2 * MF * MB], F16)
        vr32 = vr[:, :].bitcast(F32)
        qkv_tok = vr32[:, 0:2 * 3 * D].rearrange("p (s n) -> p s n", s=2)
        qkv_head = vr32[:, 0:RING * 4 * (HC + 1)].rearrange("p (s k c) -> p s k c", s=RING, k=4)
        gh = vr[:, 0:MF * MB].rearrange("p (m t) -> p m t", m=MF)
        gl = vr[:, MF * MB:2 * MF * MB].rearrange("p (m t) -> p m t", m=MF)
        work = sb("work", [P, 1024 + 2 * D], F32)
        full = [work[:, 512 * j:512 * j + 512] for j in range(2)]
        gelu = [work[:, MB * j:MB * j + MB] for j in range(3)]
        norm = [work[:, 1024 + D * j:1024 + D * j + D] for j in range(2)]
        mod_rows = work[0:VECTORS * KC, 0:P]
        gates = sb("gates", [P, 2, D], F32)
        mod = sb("mod", [P, VECTORS * KC], F32)
        stats = sb("stats", [P, 4, 2, 6], F32)
        mv = sb("mv", [P, NT, 2], F32)
        rstd = sb("rstd", [P, NT], F32)
        negmax = sb("negmax", [P, 2, 4], F32)
        inv_sum = sb("inv_sum", [P, 2, 4], F32)

        ident = sb("ident", [P, P], F32)
        pick = sb("pick", [P, 3, P], F16)
        bias_rows = sb("bias_rows", [P, 3 * D], F16)
        own = sb("own", [P, P], BF16)
        others = sb("others", [P, P], BF16)
        f_bias = sb("f_bias", [P, MF], F32)
        minus_half = sb("minus_half", [P, 4], F32)
        epsilon = sb("epsilon", [P, 4], F32)
        silu_t = sb("silu_t", [P, KC, B], F32)
        ps = ctx.enter_context(nc.psum_tensor("ps", [P, 8, 512], F32))

        tok_f = tok[:, :, :].rearrange("p t d -> p (t d)")
        xr_f = xr[:, :].bitcast(F32)
        ada_stage = [tok_f[:, 0:VECTORS * D], vr32[:, 0:VECTORS * D], xr_f[:, 0:VECTORS * D]]
        w_stage = [r[:, n * MLP:n * MLP + MLP] for r in (tok_f, vr32, xr_f) for n in range(2)]
        ada_bias = w1_h[:, :, :].rearrange("p c n -> p (c n)").bitcast(F32)[0:B, 0:VECTORS * D]
        ada_out = w1_l[:, :, :].rearrange("p c n -> p (c n)").bitcast(F32)[0:B, 0:VECTORS * D]
        w2_f = w2_h[:, :, :].rearrange("p c n -> p (c n)")
        bias_f = w2_f[0:1, 0:10 * D].bitcast(F32)
        bias_h = w2_f[0:1, 10 * D:15 * D]
        w2l_h = w2_l[:, :, :].rearrange("p c n -> p (c n)")
        bias_l = w2l_h[0:1, 10 * D:15 * D]
        w2l_f = w2_l[:, :, :].rearrange("p c n -> p (c n)").bitcast(F32)
        cond_in, silu_c = w2l_f[0:B, 0:D], w2l_f[0:B, D:2 * D]
        col_rows = w2l_f[0:MF, 2 * D:2 * D + P]

        consts_set, cond_in_s, ada_b_in = (sem(n) for n in ("consts_set", "cond_in_s", "ada_b_in"))
        ada_w_in = [sem(f"ada_w_in{i}") for i in range(3)]
        rows_loaded, silu_done, silu_tr, silu_cp = (sem(n) for n in ("rows_loaded", "silu_done", "silu_tr", "silu_cp"))
        ada_mm, ada_added, mod_stored, bias_split, bias_in = (sem(n) for n in ("ada_mm", "ada_added", "mod_stored", "bias_split", "bias_in"))
        cols_tr, cols_cp = sem("cols_tr"), sem("cols_cp")
        w_in = [sem(f"w_in{i}") for i in range(STAGES)]
        w_high, w_low = sem("w_high"), sem("w_low")
        waits_passed = sem("waits_passed")
        x_in, gates_in, mod_in, mod_tr, mod_cp = (sem(n) for n in ("x_in", "gates_in", "mod_in", "mod_tr", "mod_cp"))
        stats_done, mean_done, eps_done, rstd_done, norm_done, norm_used = (
            sem(n) for n in ("stats_done", "mean_done", "eps_done", "rstd_done", "norm_done", "norm_used"))
        split_mm, full_done, high_done, low_done = (sem(n) for n in ("split_mm", "full_done", "high_done", "low_done"))
        qkv_mm = [sem("qkv_mm0"), sem("qkv_mm1")]
        qkv_done = [sem("qkv_done0"), sem("qkv_done1")]
        qkv_stored = [sem("qkv_stored0"), sem("qkv_stored1")]
        ones_set = sem("ones_set")
        heads_in = [sem(f"heads_in{i}") for i in range(RING // 2)]
        qk_turned, q_copied, k_copied, scores_mm, max_done, shifted, exp_done = (
            sem(n) for n in ("qk_turned", "q_copied", "k_copied", "scores_mm", "max_done", "shifted", "exp_done"))
        probs_turned, probs_copied, out_mm, inv_done, out_done = (
            sem(n) for n in ("probs_turned", "probs_copied", "out_mm", "inv_done", "out_done"))
        xres_in = [sem("xres_in0"), sem("xres_in1")]
        proj_mm, proj_gated, x1_done = (sem(n) for n in ("proj_mm", "proj_gated", "x1_done"))
        fc1_mm, gelu_done, g_high, g_low, fc2_mm, mlp_gated, x2_done, stored = (
            sem(n) for n in ("fc1_mm", "gelu_done", "g_high", "g_low", "fc2_mm", "mlp_gated", "x2_done", "stored"))

        jobs = []
        for w, h, l, n in ((qkv_w, wq_h, wq_l, 3 * D), (fc1_w, w1_h, w1_l, MLP)):
            for c in range(KF):
                jobs.append((w[c * P:(c + 1) * P, :], h[:, c, :], l[:, c, :], n, False))
            jobs.append((w[KF * P:D, :], h[:, KF, :], l[:, KF, :], n, True))
        jobs.append((proj_w[0:KF * P, :].rearrange("(c p) n -> p c n", p=P), wp_h[:, 0:KF, :], wp_l[:, 0:KF, :], KF * D, False))
        jobs.append((proj_w[KF * P:D, :], wp_h[:, KF, :], wp_l[:, KF, :], D, True))
        for c in range(0, MF, 4):
            k = min(4, MF - c)
            jobs.append((fc2_w[c * P:(c + k) * P, :].rearrange("(c p) n -> p c n", p=P), w2_h[:, c:c + k, :], w2_l[:, c:c + k, :], k * D, False))
        W1_JOB, W2_JOB = KC, 2 * KC + 2

        def stage_of(j):
            _, h, _, n, _ = jobs[j]
            s = w_stage[j % STAGES][:, 0:n]
            return s if len(h.shape) == 2 else s.rearrange("p (c n) -> p c n", n=D)

        by_head = lambda a: a.rearrange("p (k h d) -> p k h d", k=3, d=DH)
        of_head = lambda a: a.rearrange("p (h k d) -> p k h d", k=3, d=DH)

        block = ctx.enter_context(nc.Block())

        def before(b, per, j, ring):
            return b * per + (max(0, j - ring + 1) if isinstance(j, int) else j - (ring - 1))

        def pipeline(engine, body):
            for i in range(RING):
                body(i, i, lambda lag: i >= lag)
            with engine.Fori(0, GROUPS // RING - 1) as r:
                for n in range(RING):
                    body(r * RING + (RING + n), n, lambda lag: True)
            for i in range(GROUPS, GROUPS + LAGS):
                body(i, i % RING, lambda lag: i - lag < GROUPS)

        def passed(engine):
            engine.sem_inc(waits_passed, 1)

        @block.sync
        def _(sp):
            sp.dma_start(cond_in, cond).then_inc(cond_in_s, 16)
            sp.dma_start(ada_bias, ada_b.rearrange("(a n) -> a n", a=1).broadcast_to([B, VECTORS * D])).then_inc(ada_b_in, 16)
            sp.dma_start(col_rows, fc1_b.rearrange("(m p) -> m p", p=P)).then_inc(rows_loaded, 16)
            for k in range(3):
                sp.dma_start(of_head(bias_f[:, 0:3 * D])[:, k], by_head(qkv_b.rearrange("(a n) -> a n", a=1))[:, k]).then_inc(rows_loaded, 16)
            for i, v in enumerate((proj_b, fc2_b)):
                sp.dma_start(bias_f[:, (3 + i) * D:(4 + i) * D], v.rearrange("(a n) -> a n", a=1)).then_inc(rows_loaded, 16)
            for k in range(KC):
                rows = min(P, D - k * P)
                if k >= 3:
                    sp.wait_ge(ada_mm, k - 2)
                sp.dma_start(ada_stage[k % 3][0:rows, :], ada_w[k * P:k * P + rows, :]).then_inc(ada_w_in[k % 3], 16)
            sp.wait_ge(consts_set, BIAS_SET)
            sp.wait_ge(bias_split, 2)
            for i, (at, n) in enumerate(((0, 3 * D), (3 * D, D), (4 * D, D))):
                sp.dma_start(bias_rows[32 * i:32 * i + 1, 0:n], bias_h[:, at:at + n]).then_inc(bias_in, 16)
                sp.dma_start(bias_rows[32 * i + 1:32 * i + 2, 0:n], bias_l[:, at:at + n]).then_inc(bias_in, 16)
            sp.wait_ge(ada_added, 1)
            ada_v = ada_out.rearrange("b (v d) -> b v d", v=VECTORS)
            sp.dma_start(mod_dram[:, :, 0:D], ada_v).then_inc(mod_stored, 16)
            sp.dma_start(mod_dram[:, :, D:KC * P], ada_v[:, :, KF * P:D]).then_inc(mod_stored, 16)
            sp.wait_ge(ada_mm, KC)
            sp.wait_ge(mod_stored, 32)
            sp.wait_ge(bias_in, 16 * 6)
            sp.wait_ge(cols_tr, 1)
            for j, (src, h, l, n, last) in enumerate(jobs):
                if j >= STAGES:
                    sp.wait_ge(w_low, j - STAGES + 1)
                dst = stage_of(j)
                if last:
                    sp.dma_start(dst[0:REM], src).then_inc(w_in[j % STAGES], 16)
                    sp.dma_start(dst[REM:P], src).then_inc(w_in[j % STAGES], 16)
                else:
                    sp.dma_start(dst[0:REM], src[0:REM]).then_inc(w_in[j % STAGES], 16)
                    sp.dma_start(dst[REM:P], src[REM:P]).then_inc(w_in[j % STAGES], 16)
            sp.wait_ge(w_low, len(jobs))

            with sp.Fori(0, B) as b:
                sp.wait_ge(x2_done, b * NT)
                sp.dma_start(mod_rows, mod_dram[bass.ds(b, 1), :, :].rearrange("b v (c p) -> (b v c) p", p=P)).then_inc(mod_in, 16)
                for i, v in enumerate((GATE_MSA, GATE_MLP)):
                    sp.dma_start(gates[:, i, :], mod_dram[bass.ds(b, 1), v, 0:D].broadcast_to([P, D])).then_inc(gates_in, 16)
                sp.wait_ge(stored, b * (NT * 16))
                sp.dma_start(tok[:, :, :], x[bass.ds(b, 1), :, :].rearrange("b (t p) d -> p (b t) d", p=P)).then_inc(x_in, 16)

                with sp.Fori(0, NT // 2) as i:
                    for u in range(2):
                        for k in range(2):
                            sp.wait_ge(qkv_done[k], b * NT + i * 2 + (u + 1))
                        sp.dma_start(qkv_dram[bass.ds(i * (2 * P) + u * P, P), :], qkv_tok[:, u, :]).then_inc(qkv_stored[u], 16)
                for u in range(2):
                    sp.wait_ge(qkv_stored[u], (b + 1) * (NT // 2 * 16))
                sp.wait_ge(ones_set, b + 1)
                by_e = qkv_dram.rearrange("(e k) (h c) -> e h k c", e=E, c=HC)

                def load_heads(w, s):
                    dst = qkv_head[:, 2 * s:2 * s + 2, :, 0:HC].rearrange("p s k c -> p (s k) c")
                    for e in range(E):
                        sp.dma_start(dst[e:P:E], by_e[e, :, bass.ds(w * 8, 8), :]).then_inc(heads_in[s], 16)

                for s in range(RING // 2):
                    load_heads(s, s)
                with sp.Fori(0, GROUPS // RING - 1) as r:
                    for s in range(RING // 2):
                        w = r * (RING // 2) + (RING // 2 + s)
                        sp.wait_ge(out_mm, b * GROUPS + w * 2 - (RING - 2))
                        load_heads(w, s)

                x_rows = x[bass.ds(b, 1), :, :].rearrange("b (p i) d -> p (b i) d", i=NT)
                sp.wait_ge(low_done, b * SPLITS + S_LN2)
                passed(sp)
                with sp.Fori(0, NT // 2) as i:
                    for u in range(2):
                        sp.wait_ge(x1_done, b * NT + i * 2)
                        sp.dma_start(norm[u].rearrange("p (i d) -> p i d", i=1), x_rows[:, bass.ds(i * 2 + u, 1), :]).then_inc(xres_in[u], 16)

                with sp.Fori(0, NT) as t:
                    sp.wait_ge(x2_done, b * NT + t + 1)
                    sp.dma_start(out[bass.ds(b, 1), :, :].rearrange("b (p i) d -> p (b i) d", i=NT)[:, bass.ds(t, 1), :],
                                 tok[:, bass.ds(t, 1), :]).then_inc(stored, 16)
            sp.wait_ge(stored, B * NT * 16)

        @block.gpsimd
        def _(pool):
            def constant(write, n):
                write.then_inc(consts_set, 1)
                pool.wait_ge(consts_set, n)

            constant(pool.memset(ident[:, :], 0.0), 1)
            constant(pool.affine_select(out=ident[:, :], in_=ident[:, :], compare_op=ALU.not_equal, fill=1.0, base=0,
                                        pattern=[[-1, P]], channel_multiplier=1), IDENT_SET)
            constant(pool.memset(bias_rows[:, :], 0.0), BIAS_SET)
            constant(pool.memset(minus_half[:, :], -0.5), 4)
            constant(pool.memset(epsilon[:, :], EPS), 5)
            constant(pool.memset(own[:, :], 0.0), 6)
            constant(pool.affine_select(out=own[:, :], in_=own[:, :], compare_op=ALU.not_equal, fill=1.0, base=0,
                                        pattern=[[0, HEADS], [-1, E]], channel_multiplier=1), 7)
            constant(pool.memset(pick[:, :, :], 0.0), 8)
            for i in range(3):
                constant(pool.memset(pick[32 * i:32 * i + 2, i, :], 1.0), 9 + i)
            constant(pool.memset(wq_l[REM:P, KF, :], 0.0), 12)
            constant(pool.memset(wp_l[REM:P, KF, :], 0.0), 13)
            constant(pool.memset(others[:, :], 0.0), 14)
            constant(pool.memset(others[0:E, :], OFF), 15)
            constant(pool.affine_select(out=others[0:E, :], in_=others[0:E, :], compare_op=ALU.not_equal, fill=0.0, base=0,
                                        pattern=[[0, HEADS], [-1, E]], channel_multiplier=1), 16)
            pool.wait_ge(mod_stored, 32)
            constant(pool.memset(w1_l[REM:P, KF, :], 0.0), CONSTANTS_SET)

            with pool.Fori(0, B) as b:
                def deviations(g):
                    t = g % NG * 4
                    pool.wait_ge(mean_done, b * (2 * NG) + g + 1)
                    pool.wait_ge(low_done, b * SPLITS + (S_LN1 if g < NG else S_LN2) + g % NG * KC)
                    pool.tensor_tensor(rstd[:, t:t + 4], mv[:, t:t + 4, 1], epsilon[:, :], ALU.add).then_inc(eps_done, 1)
                    pool.wait_ge(eps_done, b * (2 * NG) + g + 1)
                    pool.tensor_tensor(rstd[:, t:t + 4], rstd[:, t:t + 4], minus_half[:, :], ALU.pow).then_inc(rstd_done, 1)

                def low_part(j, c, n):
                    pool.wait_ge(high_done, b * SPLITS + j + 1)
                    pool.wait_ge(low_done, b * SPLITS + j)
                    s = full[j % 2]
                    at = slice(n * 512, (n + 1) * 512)
                    if c < KF:
                        pool.tensor_tensor(xl[:, c, at], s, xh[:, c, at], ALU.subtract).then_inc(low_done, 1)
                    else:
                        pool.tensor_tensor(xh[REM:P, c, at], s[REM:P], xh[REM:P, c, at], ALU.subtract).then_inc(low_done, 1)

                for g in range(NG):
                    deviations(g)
                    for c in range(KC):
                        low_part(S_LN1 + g * KC + c, c, g)
                for u in range(2):
                    pool.wait_ge(qkv_stored[u], (b + 1) * (NT // 2 * 16))
                passed(pool)
                pool.memset(qkv_head[:, :, :, HC:HC + 1], 1.0).then_inc(ones_set, 1)
                for g in range(NG):
                    for c in range(KC):
                        low_part(S_ATT + g * KC + c, c, g)
                for g in range(NG):
                    deviations(NG + g)
                    for c in range(KC):
                        low_part(S_LN2 + g * KC + c, c, g)

        @block.scalar
        def _(act):
            act.wait_ge(cond_in_s, 16)
            act.activation(silu_c, cond_in, ACT.Silu).then_inc(silu_done, 1)
            for j, (src, h, l, n, last) in enumerate(jobs):
                act.wait_ge(w_in[j % STAGES], 32 * (j // STAGES + 1))
                if j < W1_JOB:
                    h, stage = of_head(h), by_head(stage_of(j))
                    for k in range(3):
                        last_write = act.activation(h[:, k], stage[:, k], ACT.Copy, scale=WSCALE)
                    last_write.then_inc(w_high, 1)
                else:
                    act.activation(h, stage_of(j), ACT.Copy, scale=WSCALE).then_inc(w_high, 1)

            with act.Fori(0, B) as b:
                def high_part(j, c, n):
                    act.wait_ge(full_done, b * SPLITS + j + 1)
                    act.activation(xh[:, c, n * 512:(n + 1) * 512], full[j % 2], ACT.Copy).then_inc(high_done, 1)

                for g in range(NG):
                    for c in range(KC):
                        high_part(S_LN1 + g * KC + c, c, g)
                with act.Fori(0, NT // 2) as i:
                    for u in range(2):
                        act.wait_ge(qkv_mm[0], b * NT + i * 2 + (u + 1))
                        act.wait_ge(qkv_stored[u], b * (NT // 2 * 16) + i * 16)
                        act.activation(qkv_tok[:, u, 0:2 * QC].rearrange("p (k n) -> p k n", k=2), ps[:, 4 * u:4 * u + 2, 0:QC],
                                       ACT.Copy, scale=1 / WSCALE).then_inc(qkv_done[0], 1)

                def attend(i, n, live):
                    G = b * GROUPS + i
                    if live(0):
                        act.wait_ge(qk_turned, G + 1)
                        act.wait_ge(scores_mm, before(b, GROUPS, i, 2))
                        act.activation(q_t[0:DH, n % 2, :], ps[0:DH, 0, :], ACT.Copy, scale=SCALE).then_inc(q_copied, 1)
                        act.activation(k_t[0:DH, n % 2, :], ps[0:DH, 1, :], ACT.Copy).then_inc(k_copied, 1)
                    if live(1):
                        act.wait_ge(shifted, G)
                        act.activation(probs[:, (n - 1) % 2, :], probs[:, (n - 1) % 2, :], ACT.Exp).then_inc(exp_done, 1)
                    if live(2):
                        act.wait_ge(probs_turned, G - 1)
                        act.wait_ge(out_mm, before(b, GROUPS, i - 2, 2))
                        act.activation(probs_t[:, n % 2, :], ps[:, 4 + n % 2, :], ACT.Copy).then_inc(probs_copied, 1)

                pipeline(act, attend)

                for g in range(NG):
                    for c in range(KC):
                        high_part(S_ATT + g * KC + c, c, g)
                for g in range(NG):
                    for c in range(KC):
                        high_part(S_LN2 + g * KC + c, c, g)
                with act.Fori(0, NB) as q:
                    for m in range(MF):
                        if m == 0:
                            act.wait_ge(low_done, (b + 1) * SPLITS)
                        act.wait_ge(fc1_mm, b * (NB * MF) + q * MF + (m + 1))
                        act.wait_ge(g_low, b * (NB * MF) + q * MF + max(0, m - 2))
                        act.activation(gelu[m % 3], ps[:, m % 3, 0:MB], ACT.Gelu, bias=f_bias[:, m:m + 1],
                                       scale=1 / WSCALE).then_inc(gelu_done, 1)

        @block.vector
        def _(dve):
            dve.wait_ge(silu_tr, 1)
            dve.tensor_copy(silu_t[:, 0:KF, :], ps[:, 7, 0:KF * B].rearrange("p (k b) -> p k b", b=B)).then_inc(silu_cp, 1)
            dve.tensor_copy(silu_t[0:REM, KF, :], ps[0:REM, 7, KF * B:KC * B]).then_inc(silu_cp, 1)
            dve.wait_ge(cols_tr, 1)
            dve.tensor_copy(f_bias[:, :], ps[:, 7, 64:64 + MF]).then_inc(cols_cp, 1)
            dve.wait_ge(rows_loaded, 16 * 6)
            dve.tensor_scalar(bias_h, bias_f, WSCALE, None, ALU.mult).then_inc(bias_split, 1)
            dve.wait_ge(bias_split, 1)
            dve.scalar_tensor_tensor(out=bias_l, in0=bias_f, scalar=WSCALE, in1=bias_h, op0=ALU.mult, op1=ALU.subtract).then_inc(bias_split, 1)
            dve.wait_ge(ada_mm, KC)
            dve.wait_ge(ada_b_in, 16)
            full_banks = VECTORS * D // 512
            dve.tensor_tensor(ada_out[:, 0:full_banks * 512].rearrange("b (k n) -> b k n", n=512), ps[0:B, 0:full_banks, :],
                              ada_bias[:, 0:full_banks * 512].rearrange("b (k n) -> b k n", n=512), ALU.add)
            rest = VECTORS * D - full_banks * 512
            dve.tensor_tensor(ada_out[:, full_banks * 512:], ps[0:B, full_banks, 0:rest], ada_bias[:, full_banks * 512:], ALU.add).then_inc(ada_added, 1)
            for j, (src, h, l, n, last) in enumerate(jobs):
                dve.wait_ge(w_high, j + 1)
                r = slice(0, REM if last else P)
                if j < W1_JOB:
                    for k in range(3):
                        last_write = dve.scalar_tensor_tensor(out=of_head(l[r])[:, k], in0=by_head(stage_of(j)[r])[:, k], scalar=WSCALE,
                                                              in1=of_head(h[r])[:, k], op0=ALU.mult, op1=ALU.subtract)
                    last_write.then_inc(w_low, 1)
                else:
                    dve.scalar_tensor_tensor(out=l[r], in0=stage_of(j)[r], scalar=WSCALE, in1=h[r], op0=ALU.mult, op1=ALU.subtract).then_inc(w_low, 1)

            with dve.Fori(0, B) as b:
                def normalize(g, first):
                    t0 = g % NG * 4
                    for t in range(4):
                        for k in range(2):
                            last = dve.bn_stats(stats[:, t, k, :], tok[:, t0 + t, k * HALF:(k + 1) * HALF])
                    last.then_inc(stats_done, 1)
                    dve.wait_ge(stats_done, b * (2 * NG) + g + 1)
                    passed(dve)
                    for t in range(4):
                        last = dve.bn_aggr(mv[:, t0 + t, :], stats[:, t, :, :])
                    last.then_inc(mean_done, 1)
                    dve.wait_ge(mean_done, b * (2 * NG) + g + 1)
                    dve.wait_ge(rstd_done, b * (2 * NG) + g + 1)
                    for t in range(4):
                        if t >= 2:
                            dve.wait_ge(norm_used, b * (4 * NG) + g * 2 + t - 1)
                        dve.tensor_scalar(norm[t % 2], tok[:, t0 + t, :], mv[:, t0 + t, 0:1], rstd[:, t0 + t:t0 + t + 1],
                                          ALU.subtract, ALU.mult).then_inc(norm_done, 1)

                def full_value(j, c, shift):
                    dve.wait_ge(split_mm, b * SPLITS + j + 1)
                    dve.wait_ge(low_done, before(b, SPLITS, j, 2))
                    if shift is None:
                        dve.tensor_scalar(full[j % 2], ps[:, c, :], 1.0, None, ALU.mult).then_inc(full_done, 1)
                    else:
                        dve.tensor_scalar(full[j % 2], ps[:, c, :], mod[:, (shift + 1) * KC + c:(shift + 1) * KC + c + 1],
                                          mod[:, shift * KC + c:shift * KC + c + 1], ALU.mult, ALU.add).then_inc(full_done, 1)

                dve.wait_ge(mod_tr, b + 1)
                dve.tensor_copy(mod[:, :], ps[:, 7, 0:VECTORS * KC]).then_inc(mod_cp, 1)
                dve.wait_ge(mod_cp, b * 4 + 1)
                dve.wait_ge(gates_in, (b + 1) * 32)
                for v in (SCALE_MSA, SCALE_MLP):
                    dve.tensor_scalar(mod[:, v * KC:(v + 1) * KC], mod[:, v * KC:(v + 1) * KC], 1.0, None, ALU.add).then_inc(mod_cp, 1)
                dve.tensor_scalar(gates[:, :, :], gates[:, :, :], 1 / WSCALE, None, ALU.mult).then_inc(mod_cp, 1)
                dve.wait_ge(mod_cp, (b + 1) * 4)
                dve.wait_ge(x_in, (b + 1) * 16)
                for g in range(NG):
                    normalize(g, True)
                    for c in range(KC):
                        full_value(S_LN1 + g * KC + c, c, SHIFT_MSA)
                with dve.Fori(0, NT // 2) as i:
                    for u in range(2):
                        dve.wait_ge(qkv_mm[1], b * NT + i * 2 + (u + 1))
                        dve.wait_ge(qkv_stored[u], b * (NT // 2 * 16) + i * 16)
                        dve.tensor_scalar(qkv_tok[:, u, 2 * QC:4 * QC].rearrange("p (k n) -> p k n", k=2),
                                          ps[:, 4 * u + 2:4 * u + 4, 0:QC], 1 / WSCALE, None, ALU.mult).then_inc(qkv_done[1], 1)

                def attend(i, n, live):
                    G = b * GROUPS + i
                    if live(1):
                        s = (n - 1) % 2
                        scores = ps[:, 2 + s, :].rearrange("p (k c) -> p k c", k=4)
                        dve.wait_ge(scores_mm, G)
                        dve.tensor_reduce(negmax[:, s, :], scores, AX.X, ALU.max, negate=True).then_inc(max_done, 1)
                        dve.wait_ge(max_done, G)
                        dve.wait_ge(probs_turned, before(b, GROUPS, i - 1, 2))
                        dve.tensor_tensor(probs[:, s, :].rearrange("p (k c) -> p k c", k=4), scores,
                                          negmax[:, s, :].unsqueeze(2).broadcast_to([P, 4, P]), ALU.add).then_inc(shifted, 1)
                    if live(3):
                        s = (n - 3) % 2
                        o = ps[:, 6 + s, 0:4 * (DH + 1)].rearrange("p (k c) -> p k c", k=4)
                        dve.wait_ge(out_mm, G - 2)
                        dve.reciprocal(inv_sum[:, s, :], o[:, :, DH]).then_inc(inv_done, 1)
                        dve.wait_ge(inv_done, G - 2)
                        dve.tensor_tensor(tok_f[:, bass.ds((i - 3) * (4 * DH), 4 * DH)].rearrange("p (k c) -> p k c", k=4),
                                          o[:, :, 0:DH], inv_sum[:, s, :].unsqueeze(2).broadcast_to([P, 4, DH]), ALU.mult).then_inc(out_done, 1)

                pipeline(dve, attend)

                for g in range(NG):
                    for c in range(KC):
                        full_value(S_ATT + g * KC + c, c, None)
                with dve.Fori(0, NT // 2) as i:
                    for u in range(2):
                        t = i * 2 + u
                        row = tok[:, bass.ds(t, 1), :].rearrange("p t (k n) -> p (t k) n", k=2)
                        dve.wait_ge(proj_mm, b * NT + t + 1)
                        dve.wait_ge(xres_in[u], b * (NT // 2 * 16) + i * 16 + 16)
                        dve.tensor_tensor(row, ps[:, 4 + 2 * u:6 + 2 * u, 0:HALF],
                                          gates[:, 0, :].rearrange("p (k n) -> p k n", k=2), ALU.mult).then_inc(proj_gated, 1)
                        dve.wait_ge(proj_gated, b * NT + t + 1)
                        row = tok[:, bass.ds(t, 1), :].rearrange("p t d -> p (t d)")
                        dve.tensor_tensor(row, row, norm[u], ALU.add).then_inc(x1_done, 1)
                dve.wait_ge(x1_done, (b + 1) * NT)
                for g in range(NG):
                    normalize(NG + g, False)
                    for c in range(KC):
                        full_value(S_LN2 + g * KC + c, c, SHIFT_MLP)
                with dve.Fori(0, NB) as q:
                    for m in range(MF):
                        M = b * (NB * MF) + q * MF + (m + 1)
                        dve.wait_ge(gelu_done, M)
                        if m == 0:
                            dve.wait_ge(fc2_mm, b * NT + q * 2)
                        dve.tensor_copy(gh[:, m, :], gelu[m % 3]).then_inc(g_high, 1)
                        dve.wait_ge(g_high, M)
                        dve.tensor_tensor(gl[:, m, :], gelu[m % 3], gh[:, m, :], ALU.subtract).then_inc(g_low, 1)
                    for u in range(2):
                        t = q * 2 + u
                        dve.wait_ge(fc2_mm, b * NT + t + 1)
                        dve.tensor_tensor(norm[u].rearrange("p (k n) -> p k n", k=2), ps[:, 4 + 2 * u:6 + 2 * u, 0:HALF],
                                          gates[:, 1, :].rearrange("p (k n) -> p k n", k=2), ALU.mult).then_inc(mlp_gated, 1)
                        dve.wait_ge(mlp_gated, b * NT + t + 1)
                        row = tok[:, bass.ds(t, 1), :].rearrange("p t d -> p (t d)")
                        dve.tensor_tensor(row, row, norm[u], ALU.add).then_inc(x2_done, 1)

        @block.tensor
        def _(pe):
            pe.wait_ge(silu_done, 1)
            pe.wait_ge(consts_set, IDENT_SET)
            for k in range(KC):
                n = min(P, D - k * P)
                last = pe.transpose(ps[0:n, 7, k * B:(k + 1) * B], silu_c[:, k * P:k * P + n], ident[0:B, 0:B])
            last.then_inc(silu_tr, 1)
            pe.wait_ge(silu_cp, 2)
            pe.wait_ge(rows_loaded, 16 * 6)
            pe.transpose(ps[:, 7, 64:64 + MF], col_rows, ident[0:MF, 0:MF]).then_inc(cols_tr, 1)
            for k in range(KC):
                rows = min(P, D - k * P)
                pe.wait_ge(ada_w_in[k % 3], 16 * (k // 3 + 1))
                for n in range(0, VECTORS * D, 512):
                    w = min(512, VECTORS * D - n)
                    last = pe.matmul(ps[0:B, n // 512, 0:w], silu_t[0:rows, k, :], ada_stage[k % 3][0:rows, n:n + w],
                                     start=(k == 0), stop=(k == KC - 1))
                last.then_inc(ada_mm, 1)
            pe.wait_ge(cols_cp, 1)
            pe.wait_ge(ada_added, 1)
            pe.wait_ge(w_low, len(jobs))
            pe.wait_ge(bias_in, 16 * 6)
            pe.wait_ge(consts_set, CONSTANTS_SET)

            def passes(wh, wl):
                for c in range(KC):
                    yield xh[:, c, :], wh[:, c, :]
                for c in range(KC):
                    yield xh[:, c, :], wl[:, c, :]
                for c in range(KF):
                    yield xl[:, c, :], wh[:, c, :]

            def by_tokens(t, bank, wh, wl, col, n, bias, done):
                for i, (xa, wa) in enumerate(passes(wh, wl)):
                    for k in range(2):
                        pe.matmul(ps[:, bank + k, 0:n], xa[:, bass.ds(t * P, P)], wa[:, col + k * n:col + (k + 1) * n],
                                  start=(i == 0), stop=False)
                for k in range(2):
                    last = pe.matmul(ps[:, bank + k, 0:n], pick[:, bias, :], bias_rows[:, col + k * n:col + (k + 1) * n],
                                     start=False, stop=True)
                last.then_inc(done, 1)

            with pe.Fori(0, B) as b:
                def turn(g, j0, normalized):
                    t0 = g % NG * 4
                    if g % NG:
                        pe.wait_ge(full_done, b * SPLITS + j0)
                    for t in range(4):
                        if normalized:
                            pe.wait_ge(norm_done, b * (2 * NT) + g * 4 + t + 1)
                        src = norm[t % 2] if normalized else tok[:, t0 + t, :]
                        at = slice(t * P, (t + 1) * P)
                        for c in range(KF):
                            last = pe.transpose(ps[:, c, at], src[:, c * P:(c + 1) * P], ident[:, :])
                            if t == 3:
                                last.then_inc(split_mm, 1)
                        pe.transpose(ps[:, KF, at], src[:, D - P:D], ident[:, :])
                        last = pe.transpose(ps[0:REM, KF, at], src[:, KF * P:D], ident[:, :])
                        if t == 3:
                            last.then_inc(split_mm, 1)
                        if normalized and t < 2:
                            last.then_inc(norm_used, 1)

                pe.wait_ge(mod_in, (b + 1) * 16)
                pe.wait_ge(x2_done, b * NT)
                passed(pe)
                pe.transpose(ps[:, 7, 0:VECTORS * KC], mod_rows, ident[0:VECTORS * KC, 0:VECTORS * KC]).then_inc(mod_tr, 1)
                for g in range(NG):
                    turn(g, S_LN1 + g * KC, True)

                pe.wait_ge(low_done, b * SPLITS + S_ATT)
                passed(pe)
                with pe.Fori(0, NT // 2) as i:
                    for u in range(2):
                        for k in range(2):
                            pe.wait_ge(qkv_done[k], b * NT + i * 2 + max(0, u - 1))
                            by_tokens(i * 2 + u, 4 * u + 2 * k, wq_h, wq_l, k * 2 * QC, QC, 0, qkv_mm[k])
                for k in range(2):
                    pe.wait_ge(qkv_done[k], (b + 1) * NT)
                passed(pe)

                def attend(i, n, live):
                    G = b * GROUPS + i
                    if live(0):
                        pe.wait_ge(heads_in[n // 2], b * (GROUPS // RING * 128) + (i - n) * 16 + 128)
                        pe.wait_ge(k_copied, G)
                        passed(pe)
                        for part in range(2):
                            for k in range(4):
                                last = pe.transpose(ps[0:DH, part, k * P:(k + 1) * P], qkv_head[:, n, k, part * DH:(part + 1) * DH], ident[:, :])
                        last.then_inc(qk_turned, 1)
                    if live(2):
                        s = n % 2
                        pe.wait_ge(exp_done, G - 1)
                        pe.wait_ge(probs_copied, before(b, GROUPS, i - 2, 2))
                        for k in range(4):
                            last = pe.transpose(ps[:, 4 + s, k * P:(k + 1) * P], probs[:, s, k * P:(k + 1) * P], ident[:, :])
                        last.then_inc(probs_turned, 1)
                    if live(3):
                        s = (n - 3) % 2
                        pe.wait_ge(probs_copied, G - 2)
                        pe.wait_ge(out_done, before(b, GROUPS, i - 3, 2))
                        for k in range(4):
                            last = pe.matmul(ps[:, 6 + s, k * (DH + 1):(k + 1) * (DH + 1)], probs_t[:, s, k * P:(k + 1) * P],
                                             qkv_head[:, (n - 3) % RING, k, 2 * DH:], start=True, stop=True)
                        last.then_inc(out_mm, 1)
                    if live(1):
                        s = (n - 1) % 2
                        pe.wait_ge(k_copied, G)
                        pe.wait_ge(shifted, before(b, GROUPS, i - 1, 2))
                        pe.matmul(ps[:, 2 + s, :].rearrange("p (k c) -> p k c", k=4), own[:, :],
                                  others[:, :].unsqueeze(1).broadcast_to([P, 4, P]), start=True, stop=False)
                        for k in range(4):
                            last = pe.matmul(ps[:, 2 + s, k * P:(k + 1) * P], q_t[0:DH, s, k * P:(k + 1) * P], k_t[0:DH, s, k * P:(k + 1) * P],
                                             start=False, stop=(k == 3))
                        last.then_inc(scores_mm, 1)

                pipeline(pe, attend)

                pe.wait_ge(out_done, (b + 1) * GROUPS)
                for g in range(NG):
                    turn(g, S_ATT + g * KC, False)
                pe.wait_ge(low_done, b * SPLITS + S_LN2)
                passed(pe)
                with pe.Fori(0, NT // 2) as i:
                    for u in range(2):
                        pe.wait_ge(proj_gated, b * NT + i * 2)
                        by_tokens(i * 2 + u, 4 + 2 * u, wp_h, wp_l, 0, HALF, 1, proj_mm)
                for g in range(NG):
                    turn(NG + g, S_LN2 + g * KC, True)

                pe.wait_ge(low_done, (b + 1) * SPLITS)
                pe.wait_ge(proj_gated, (b + 1) * NT)
                passed(pe)
                with pe.Fori(0, NB) as q:
                    for m in range(MF):
                        pe.wait_ge(gelu_done, b * (NB * MF) + q * MF + max(0, m - 2))
                        ops = list(passes(w1_h, w1_l))
                        for i, (xa, wa) in enumerate(ops):
                            last = pe.matmul(ps[:, m % 3, 0:MB], wa[:, m * P:(m + 1) * P], xa[:, bass.ds(q * MB, MB)],
                                             start=(i == 0), stop=(i == len(ops) - 1))
                        last.then_inc(fc1_mm, 1)
                    for u in range(2):
                        pe.wait_ge(mlp_gated, b * NT + q * 2)
                        at = slice(u * P, (u + 1) * P)
                        for m in range(MF):
                            if u == 0:
                                pe.wait_ge(g_low, b * (NB * MF) + q * MF + (m + 1))
                            for i, (ga, wa) in enumerate(((gh, w2_h), (gh, w2_l), (gl, w2_h))):
                                for k in range(2):
                                    pe.matmul(ps[:, 4 + 2 * u + k, 0:HALF], ga[:, m, at], wa[:, m, k * HALF:(k + 1) * HALF],
                                              start=(m == 0 and i == 0), stop=False)
                        for k in range(2):
                            last = pe.matmul(ps[:, 4 + 2 * u + k, 0:HALF], pick[:, 2, :], bias_rows[:, k * HALF:(k + 1) * HALF],
                                             start=False, stop=True)
                        last.then_inc(fc2_mm, 1)


_INS = ['x', 'cond_1152', 'L0_cond_qkv_w', 'L0_cond_qkv_b', 'L0_cond_proj_w', 'L0_cond_proj_b', 'L0_cond_fc1_w',
        'L0_cond_fc1_b', 'L0_cond_fc2_w', 'L0_cond_fc2_b', 'L0_cond_ada_w', 'L0_cond_ada_b']
_OUTS = [((8, 1024, 576), 'float32')]


def kernel(**inputs):
    import numpy as _np
    import concourse.bacc as _bacc
    from concourse import mybir as _mybir
    from concourse.bass_utils import run_bass_kernel_spmd as _run

    nc = _bacc.Bacc("TRN2", target_bir_lowering=False, num_devices=1)
    arrays, args = {}, []
    for name in _INS:
        a = _np.ascontiguousarray(inputs[name])
        arrays[f"in_{name}_dram"] = a
        args.append(nc.dram_tensor(f"in_{name}_dram", a.shape, _mybir.dt.from_np(a.dtype), kind="ExternalInput").ap())
    for i, (shape, dtype) in enumerate(_OUTS):
        dt = _mybir.dt.from_np(_np.dtype(dtype))
        args.append(nc.dram_tensor(f"out_{i}_dram", shape, dt, kind="ExternalOutput").ap())
    block_kernel(nc, *args)
    r = _run(nc, [arrays], core_ids=[0])
    got = tuple(r.results[0][f"out_{i}_dram"] for i in range(len(_OUTS)))
    return got[0]
```

```python
from contextlib import ExitStack

import concourse.bass as bass
from concourse import mybir

F32 = mybir.dt.float32
F16 = mybir.dt.float16
BF16 = mybir.dt.bfloat16
ALU = mybir.AluOpType
ACT = mybir.ActivationFunctionType
AX = mybir.AxisListType

P = 128
HEADS = 16
EPS = 1e-6
WSCALE = 256.0
QSCALE = 16.0
OFF = -1e30
RING = 8
LAGS = 4
VECTORS = 6
SHIFT_MSA, SCALE_MSA, GATE_MSA, SHIFT_MLP, SCALE_MLP, GATE_MLP = range(VECTORS)
STAGES = 6
IDENT_SET, BIAS_SET, CONSTANTS_SET = 2, 3, 18


def block_kernel(nc, x, cond, qkv_w, qkv_b, proj_w, proj_b, fc1_w, fc1_b, fc2_w, fc2_b, ada_w, ada_b, out):
    B, T, D = x.shape
    DH = D // HEADS
    MLP = fc1_w.shape[1]
    NT = T // P
    NG = NT // 4
    KC = -(-D // P)
    KF = D // P
    REM = D - KF * P
    MF = MLP // P
    HALF = D // 2
    MB = 256
    NB = T // MB
    SCALE = DH ** -0.5
    E = P // HEADS
    NBLK = T // E
    GROUPS = NBLK // 4
    QL, KH, VL, VH = 0, 3 * DH, 6 * DH, 7 * DH
    HC = 8 * DH
    HP = HC + 2
    TB = P // E
    QC = 3 * D // 4
    SPLITS = NG * KC * 3
    S_LN1, S_ATT, S_LN2 = 0, NG * KC, 2 * NG * KC
    assert REM == 64 and MF % 3 == 0 and SPLITS % 2 == 0 and NBLK == P and E == NT and GROUPS % RING == 0

    with ExitStack() as ctx:
        def sb(name, shape, dt):
            return ctx.enter_context(nc.sbuf_tensor(name, shape, dt))

        def sem(name):
            return ctx.enter_context(nc.semaphore(name))

        qkv_dram = nc.dram_tensor("qkv", (T, HEADS * HC), F16).ap()
        mod_dram = nc.dram_tensor("modulation", (B, VECTORS, KC * P), F32).ap()

        wq_h, wq_l = sb("wq_h", [P, KC, 3 * D], F16), sb("wq_l", [P, KC, 3 * D], F16)
        wp_h, wp_l = sb("wp_h", [P, KC, D], F16), sb("wp_l", [P, KC, D], F16)
        w1_h, w1_l = sb("w1_h", [P, KC, MLP], F16), sb("w1_l", [P, KC, MLP], F16)
        w2_h, w2_l = sb("w2_h", [P, MF, D], F16), sb("w2_l", [P, MF, D], F16)

        tok = sb("tok", [P, NT, D], F32)
        xr = sb("xr", [P, (2 * KC - 1) * T], F16)
        xh = xr[:, 0:KC * T].rearrange("p (c t) -> p c t", c=KC)
        xl = xr[:, KC * T:].rearrange("p (c t) -> p c t", c=KC - 1)
        qk_t = xr[:, 0:2048].rearrange("p (s k t) -> p s k t", s=2, k=2)
        probs = xr[:, 2048:4096].bitcast(F32).rearrange("p (s t) -> p s t", s=2)
        probs_h = xr[:, 4096:6144].rearrange("p (s t) -> p s t", s=4)
        probs_l = xr[:, 6144:8192].rearrange("p (s t) -> p s t", s=4)
        vr = sb("vr", [P, RING * 4 * HP], F16)
        vr32 = vr[:, :].bitcast(F32)
        qkv_tok = tok[:, :, :].rearrange("p t d -> p (t d)").bitcast(F16).rearrange("p (s h c) -> p s h c", s=2, c=HC)
        qkv_head = vr[:, :].rearrange("p (s k c) -> p s k c", s=RING, k=4)
        x_res = vr32[:, 0:NT * D].rearrange("p (i d) -> p i d", i=NT)
        gh = vr[:, 0:MF * MB].rearrange("p (m t) -> p m t", m=MF)
        gl = vr[:, MF * MB:2 * MF * MB].rearrange("p (m t) -> p m t", m=MF)
        work = sb("work", [P, 1024 + 2 * D], F32)
        full = [work[:, 512 * j:512 * j + 512] for j in range(2)]
        gelu = [work[:, MB * j:MB * j + MB] for j in range(3)]
        norm = [work[:, 1024 + D * j:1024 + D * j + D] for j in range(2)]
        mod_rows = work[0:VECTORS * KC, 0:P]
        gates = sb("gates", [P, 2, D], F32)
        mod = sb("mod", [P, VECTORS * KC], F32)
        stats = sb("stats", [P, 4, 2, 6], F32)
        mv = sb("mv", [P, NT, 2], F32)
        rstd = sb("rstd", [P, NT], F32)
        negmax = sb("negmax", [P, 2, 4], F32)
        inv_sum = sb("inv_sum", [P, 2, 4], F32)

        ident = sb("ident", [P, P], F32)
        ident_h = sb("ident_h", [P, P], F16)
        pick = sb("pick", [P, 3, P], F16)
        bias_rows = sb("bias_rows", [P, 3 * D], F16)
        own = sb("own", [P, P], BF16)
        others = sb("others", [P, P], BF16)
        f_bias = sb("f_bias", [P, MF], F32)
        minus_half = sb("minus_half", [P, 4], F32)
        epsilon = sb("epsilon", [P, 4], F32)
        silu_t = sb("silu_t", [P, KC, B], F32)
        ps = ctx.enter_context(nc.psum_tensor("ps", [P, 8, 512], F32))
        ps_half = ps[:, :, :].rearrange("p k n -> p (k n)").bitcast(F16).rearrange("p (k n) -> p k n", k=8)

        tok_f = tok[:, :, :].rearrange("p t d -> p (t d)")
        xr_f = xr[:, :].bitcast(F32)
        ada_stage = [tok_f[:, 0:VECTORS * D], vr32[:, 0:VECTORS * D], xr_f[:, 0:VECTORS * D]]
        w_stage = [r[:, n * MLP:n * MLP + MLP] for r in (tok_f, vr32, xr_f) for n in range(2)]
        ada_bias = w1_h[:, :, :].rearrange("p c n -> p (c n)").bitcast(F32)[0:B, 0:VECTORS * D]
        ada_out = w1_l[:, :, :].rearrange("p c n -> p (c n)").bitcast(F32)[0:B, 0:VECTORS * D]
        w2_f = w2_h[:, :, :].rearrange("p c n -> p (c n)")
        bias_f = w2_f[0:1, 0:10 * D].bitcast(F32)
        bias_h = w2_f[0:1, 10 * D:15 * D]
        w2l_h = w2_l[:, :, :].rearrange("p c n -> p (c n)")
        bias_l = w2l_h[0:1, 10 * D:15 * D]
        w2l_f = w2_l[:, :, :].rearrange("p c n -> p (c n)").bitcast(F32)
        cond_in, silu_c = w2l_f[0:B, 0:D], w2l_f[0:B, D:2 * D]
        col_rows = w2l_f[0:MF, 2 * D:2 * D + P]

        consts_set, cond_in_s, ada_b_in = (sem(n) for n in ("consts_set", "cond_in_s", "ada_b_in"))
        ada_w_in = [sem(f"ada_w_in{i}") for i in range(3)]
        rows_loaded, silu_done, silu_tr, silu_cp = (sem(n) for n in ("rows_loaded", "silu_done", "silu_tr", "silu_cp"))
        ada_mm, ada_added, mod_stored, bias_split, bias_in = (sem(n) for n in ("ada_mm", "ada_added", "mod_stored", "bias_split", "bias_in"))
        cols_tr, cols_cp = sem("cols_tr"), sem("cols_cp")
        w_in = [sem(f"w_in{i}") for i in range(STAGES)]
        w_high, w_low = sem("w_high"), sem("w_low")
        waits_passed = sem("waits_passed")
        x_in, gates_in, mod_in, mod_tr, mod_cp = (sem(n) for n in ("x_in", "gates_in", "mod_in", "mod_tr", "mod_cp"))
        stats_done, mean_done, eps_done, rstd_done, norm_done, norm_used = (
            sem(n) for n in ("stats_done", "mean_done", "eps_done", "rstd_done", "norm_done", "norm_used"))
        split_mm, full_done, high_done, low_done = (sem(n) for n in ("split_mm", "full_done", "high_done", "low_done"))
        qkv_mm = [sem("qkv_mm0"), sem("qkv_mm1")]
        qkv_high, qkv_done = sem("qkv_high"), sem("qkv_done")
        qkv_stored = [sem("qkv_stored0"), sem("qkv_stored1")]
        ones_set = sem("ones_set")
        heads_in = [sem(f"heads_in{i}") for i in range(RING // 2)]
        qk_turned, qk_copied, scores_mm, max_done, shifted, exp_done = (
            sem(n) for n in ("qk_turned", "qk_copied", "scores_mm", "max_done", "shifted", "exp_done"))
        probs_turned, probs_high, probs_low, out_mm, inv_done, out_done = (
            sem(n) for n in ("probs_turned", "probs_high", "probs_low", "out_mm", "inv_done", "out_done"))
        xres_in = sem("xres_in")
        proj_mm, proj_gated, x1_done = (sem(n) for n in ("proj_mm", "proj_gated", "x1_done"))
        fc1_mm, gelu_done, g_high, g_low, fc2_mm, mlp_gated, x2_done, stored = (
            sem(n) for n in ("fc1_mm", "gelu_done", "g_high", "g_low", "fc2_mm", "mlp_gated", "x2_done", "stored"))

        jobs = []
        for w, h, l, n in ((qkv_w, wq_h, wq_l, 3 * D), (fc1_w, w1_h, w1_l, MLP)):
            for c in range(KF):
                jobs.append((w[c * P:(c + 1) * P, :], h[:, c, :], l[:, c, :], n, False))
            jobs.append((w[KF * P:D, :], h[:, KF, :], l[:, KF, :], n, True))
        jobs.append((proj_w[0:KF * P, :].rearrange("(c p) n -> p c n", p=P), wp_h[:, 0:KF, :], wp_l[:, 0:KF, :], KF * D, False))
        jobs.append((proj_w[KF * P:D, :], wp_h[:, KF, :], wp_l[:, KF, :], D, True))
        for c in range(0, MF, 4):
            k = min(4, MF - c)
            jobs.append((fc2_w[c * P:(c + k) * P, :].rearrange("(c p) n -> p c n", p=P), w2_h[:, c:c + k, :], w2_l[:, c:c + k, :], k * D, False))
        W1_JOB, W2_JOB = KC, 2 * KC + 2

        def stage_of(j):
            _, h, _, n, _ = jobs[j]
            s = w_stage[j % STAGES][:, 0:n]
            return s if len(h.shape) == 2 else s.rearrange("p (c n) -> p c n", n=D)

        by_head = lambda a: a.rearrange("p (k h d) -> p k h d", k=3, d=DH)
        of_head = lambda a: a.rearrange("p (h k d) -> p k h d", k=3, d=DH)

        block = ctx.enter_context(nc.Block())

        def before(b, per, j, ring):
            return b * per + (max(0, j - ring + 1) if isinstance(j, int) else j - (ring - 1))

        def pipeline(engine, body):
            for i in range(RING):
                body(i, i, lambda lag: i >= lag)
            with engine.Fori(0, GROUPS // RING - 1) as r:
                for n in range(RING):
                    body(r * RING + (RING + n), n, lambda lag: True)
            for i in range(GROUPS, GROUPS + LAGS):
                body(i, i % RING, lambda lag: i - lag < GROUPS)

        def passed(engine):
            engine.sem_inc(waits_passed, 1)

        def in_bank(u, bank):
            return slice(4 * bank, 4 * bank + 4), ps[:, 4 * u + bank, 0:QC].rearrange("p (h k d) -> p h k d", k=3, d=DH)

        @block.sync
        def _(sp):
            sp.dma_start(cond_in, cond).then_inc(cond_in_s, 16)
            sp.dma_start(ada_bias, ada_b.rearrange("(a n) -> a n", a=1).broadcast_to([B, VECTORS * D])).then_inc(ada_b_in, 16)
            sp.dma_start(col_rows, fc1_b.rearrange("(m p) -> m p", p=P)).then_inc(rows_loaded, 16)
            for k in range(3):
                sp.dma_start(of_head(bias_f[:, 0:3 * D])[:, k], by_head(qkv_b.rearrange("(a n) -> a n", a=1))[:, k]).then_inc(rows_loaded, 16)
            for i, v in enumerate((proj_b, fc2_b)):
                sp.dma_start(bias_f[:, (3 + i) * D:(4 + i) * D], v.rearrange("(a n) -> a n", a=1)).then_inc(rows_loaded, 16)
            for k in range(KC):
                rows = min(P, D - k * P)
                if k >= 3:
                    sp.wait_ge(ada_mm, k - 2)
                sp.dma_start(ada_stage[k % 3][0:rows, :], ada_w[k * P:k * P + rows, :]).then_inc(ada_w_in[k % 3], 16)
            sp.wait_ge(consts_set, BIAS_SET)
            sp.wait_ge(bias_split, 2)
            for i, (at, n) in enumerate(((0, 3 * D), (3 * D, D), (4 * D, D))):
                sp.dma_start(bias_rows[32 * i:32 * i + 1, 0:n], bias_h[:, at:at + n]).then_inc(bias_in, 16)
                sp.dma_start(bias_rows[32 * i + 1:32 * i + 2, 0:n], bias_l[:, at:at + n]).then_inc(bias_in, 16)
            sp.wait_ge(ada_added, 1)
            ada_v = ada_out.rearrange("b (v d) -> b v d", v=VECTORS)
            sp.dma_start(mod_dram[:, :, 0:D], ada_v).then_inc(mod_stored, 16)
            sp.dma_start(mod_dram[:, :, D:KC * P], ada_v[:, :, KF * P:D]).then_inc(mod_stored, 16)
            sp.wait_ge(ada_mm, KC)
            sp.wait_ge(mod_stored, 32)
            sp.wait_ge(bias_in, 16 * 6)
            sp.wait_ge(cols_tr, 1)
            for j, (src, h, l, n, last) in enumerate(jobs):
                if j >= STAGES:
                    sp.wait_ge(w_low, j - STAGES + 1)
                dst = stage_of(j)
                if last:
                    sp.dma_start(dst[0:REM], src).then_inc(w_in[j % STAGES], 16)
                    sp.dma_start(dst[REM:P], src).then_inc(w_in[j % STAGES], 16)
                else:
                    sp.dma_start(dst[0:REM], src[0:REM]).then_inc(w_in[j % STAGES], 16)
                    sp.dma_start(dst[REM:P], src[REM:P]).then_inc(w_in[j % STAGES], 16)
            sp.wait_ge(w_low, len(jobs))

            with sp.Fori(0, B) as b:
                sp.wait_ge(x2_done, b * NT)
                sp.dma_start(mod_rows, mod_dram[bass.ds(b, 1), :, :].rearrange("b v (c p) -> (b v c) p", p=P)).then_inc(mod_in, 16)
                for i, v in enumerate((GATE_MSA, GATE_MLP)):
                    sp.dma_start(gates[:, i, :], mod_dram[bass.ds(b, 1), v, 0:D].broadcast_to([P, D])).then_inc(gates_in, 16)
                sp.wait_ge(stored, b * (NB * E * 16))
                x_tiles = x[bass.ds(b, 1), :, :].rearrange("b (e t j) d -> e j (b t) d", e=E, j=TB)
                for e in range(E):
                    sp.dma_start(tok[e:P:E, :, :], x_tiles[e]).then_inc(x_in, 16)

                def store_qkv(t, u):
                    sp.wait_ge(qkv_done, b * (2 * NT) + t * 2 + 2)
                    sp.dma_start(qkv_dram[t * P:(t + 1) * P, :] if isinstance(t, int) else qkv_dram[bass.ds(t * P, P), :],
                                 qkv_tok[:, u, :, :].rearrange("p h c -> p (h c)")).then_inc(qkv_stored[u], 16)

                by_head_e = qkv_dram.rearrange("(t j e) (h c) -> (e h) t j c", e=E, j=TB, c=HC)

                def load_heads(t, s):
                    src = by_head_e[:, bass.ds(t, 1), s % 2 * 8:s % 2 * 8 + 8, :].rearrange("p t j c -> p (t j) c")
                    dst = qkv_head[:, 2 * s:2 * s + 2, :, 0:HC].rearrange("p s k c -> p (s k) c")
                    sp.dma_start(dst, src).then_inc(heads_in[s], 16)

                store_qkv(0, 0)
                store_qkv(1, 1)
                for t in range(2):
                    sp.wait_ge(qkv_stored[t], b * (NT // 2 * 16) + 16)
                    for s in (2 * t, 2 * t + 1):
                        load_heads(t, s)
                    store_qkv(2 + t, t)
                with sp.Fori(2, NT // 2) as i:
                    for u in range(2):
                        store_qkv(i * 2 + u, u)
                for u in range(2):
                    sp.wait_ge(qkv_stored[u], (b + 1) * (NT // 2 * 16))
                passed(sp)
                with sp.Fori(0, GROUPS // RING - 1) as r:
                    for s in range(RING // 2):
                        sp.wait_ge(out_mm, b * GROUPS + r * RING + (2 * s + 2))
                        load_heads(r * 2 + (2 + s // 2), s)

                x_rows = x[bass.ds(b, 1), :, :].rearrange("b (h e i) d -> e h (b i) d", e=E, i=NT)
                sp.wait_ge(out_mm, (b + 1) * GROUPS)
                for e in range(E):
                    sp.dma_start(x_res[e * HEADS:(e + 1) * HEADS], x_rows[e]).then_inc(xres_in, 16)

                out_rows = out[bass.ds(b, 1), :, :].rearrange("b (h e i) d -> e h (b i) d", e=E, i=NT)
                with sp.Fori(0, NB) as q:
                    sp.wait_ge(x2_done, b * NT + q * 2 + 2)
                    for e in range(E):
                        sp.dma_start(out_rows[e][:, bass.ds(q * 2, 2), :],
                                     tok[e * HEADS:(e + 1) * HEADS, bass.ds(q * 2, 2), :]).then_inc(stored, 16)
            sp.wait_ge(stored, B * (NB * E * 16))

        @block.gpsimd
        def _(pool):
            def constant(write, n):
                write.then_inc(consts_set, 1)
                pool.wait_ge(consts_set, n)

            constant(pool.memset(ident[:, :], 0.0), 1)
            constant(pool.affine_select(out=ident[:, :], in_=ident[:, :], compare_op=ALU.not_equal, fill=1.0, base=0,
                                        pattern=[[-1, P]], channel_multiplier=1), IDENT_SET)
            constant(pool.memset(bias_rows[:, :], 0.0), BIAS_SET)
            constant(pool.memset(minus_half[:, :], -0.5), 4)
            constant(pool.memset(epsilon[:, :], EPS), 5)
            constant(pool.memset(own[:, :], 0.0), 6)
            constant(pool.affine_select(out=own[:, :], in_=own[:, :], compare_op=ALU.not_equal, fill=1.0, base=0,
                                        pattern=[[-1, E], [0, HEADS]], channel_multiplier=1), 7)
            constant(pool.memset(pick[:, :, :], 0.0), 8)
            for i in range(3):
                constant(pool.memset(pick[32 * i:32 * i + 2, i, :], 1.0), 9 + i)
            constant(pool.memset(wq_l[REM:P, KF, :], 0.0), 12)
            constant(pool.memset(wp_l[REM:P, KF, :], 0.0), 13)
            constant(pool.memset(others[:, :], 0.0), 14)
            constant(pool.memset(others[0:E, :], OFF), 15)
            constant(pool.affine_select(out=others[0:E, :], in_=others[0:E, :], compare_op=ALU.not_equal, fill=0.0, base=0,
                                        pattern=[[-1, E], [0, HEADS]], channel_multiplier=1), 16)
            constant(pool.tensor_copy(ident_h[:, :], ident[:, :]), 17)
            pool.wait_ge(mod_stored, 32)
            constant(pool.memset(w1_l[REM:P, KF, :], 0.0), CONSTANTS_SET)

            with pool.Fori(0, B) as b:
                def deviations(g):
                    t = g % NG * 4
                    pool.wait_ge(mean_done, b * (2 * NG) + g + 1)
                    pool.wait_ge(low_done, b * SPLITS + (S_LN1 if g < NG else S_LN2) + g % NG * KC)
                    pool.tensor_tensor(rstd[:, t:t + 4], mv[:, t:t + 4, 1], epsilon[:, :], ALU.add).then_inc(eps_done, 1)
                    pool.wait_ge(eps_done, b * (2 * NG) + g + 1)
                    pool.tensor_tensor(rstd[:, t:t + 4], rstd[:, t:t + 4], minus_half[:, :], ALU.pow).then_inc(rstd_done, 1)

                def low_part(j, c, n):
                    pool.wait_ge(high_done, b * SPLITS + j + 1)
                    pool.wait_ge(low_done, b * SPLITS + j)
                    s = full[j % 2]
                    at = slice(n * 512, (n + 1) * 512)
                    if c < KF:
                        pool.tensor_tensor(xl[:, c, at], s, xh[:, c, at], ALU.subtract).then_inc(low_done, 1)
                    else:
                        pool.tensor_tensor(xh[REM:P, c, at], s[REM:P], xh[REM:P, c, at], ALU.subtract).then_inc(low_done, 1)

                for g in range(NG):
                    deviations(g)
                    for c in range(KC):
                        low_part(S_LN1 + g * KC + c, c, g)
                pool.wait_ge(low_done, b * SPLITS + S_ATT)
                pool.wait_ge(fc2_mm, b * NT)
                passed(pool)
                pool.memset(qkv_head[:, :, :, HC:HC + 1], QSCALE).then_inc(ones_set, 1)
                for g in range(NG):
                    for c in range(KC):
                        low_part(S_ATT + g * KC + c, c, g)
                for g in range(NG):
                    deviations(NG + g)
                    for c in range(KC):
                        low_part(S_LN2 + g * KC + c, c, g)

        @block.scalar
        def _(act):
            act.wait_ge(cond_in_s, 16)
            act.activation(silu_c, cond_in, ACT.Silu).then_inc(silu_done, 1)
            for j, (src, h, l, n, last) in enumerate(jobs):
                act.wait_ge(w_in[j % STAGES], 32 * (j // STAGES + 1))
                if j < W1_JOB:
                    h, stage = of_head(h), by_head(stage_of(j))
                    for k in range(3):
                        last_write = act.activation(h[:, k], stage[:, k], ACT.Copy, scale=WSCALE)
                    last_write.then_inc(w_high, 1)
                else:
                    act.activation(h, stage_of(j), ACT.Copy, scale=WSCALE).then_inc(w_high, 1)

            with act.Fori(0, B) as b:
                def high_part(j, c, n):
                    act.wait_ge(full_done, b * SPLITS + j + 1)
                    act.activation(xh[:, c, n * 512:(n + 1) * 512], full[j % 2], ACT.Copy).then_inc(high_done, 1)

                for g in range(NG):
                    for c in range(KC):
                        high_part(S_LN1 + g * KC + c, c, g)
                with act.Fori(0, NT // 2) as i:
                    for u in range(2):
                        for k in range(2):
                            act.wait_ge(qkv_mm[k], b * NT + i * 2 + (u + 1))
                            if k == 0:
                                act.wait_ge(qkv_stored[u], b * (NT // 2 * 16) + i * 16)
                            for bank in (2 * k, 2 * k + 1):
                                h, qkv = in_bank(u, bank)
                                dst = qkv_tok[:, u, h, :]
                                for part, at in enumerate((QL + DH, KH)):
                                    act.activation(dst[:, :, at:at + 2 * DH].rearrange("p h (r d) -> p h r d", r=2),
                                                   qkv[:, :, part].unsqueeze(2).broadcast_to([P, 4, 2, DH]),
                                                   ACT.Copy, scale=QSCALE / WSCALE)
                                last = act.activation(dst[:, :, VH:VH + DH], qkv[:, :, 2], ACT.Copy, scale=QSCALE / WSCALE)
                            last.then_inc(qkv_high, 1)

                def attend(i, n, live):
                    G = b * GROUPS + i
                    if live(0):
                        act.wait_ge(qk_turned, G + 1)
                        act.wait_ge(scores_mm, before(b, GROUPS, i, 2))
                        act.activation(qk_t[0:3 * DH, n % 2, :, :].rearrange("p k t -> p (k t)"), ps_half[0:3 * DH, n % 2, :],
                                       ACT.Copy).then_inc(qk_copied, 1)
                    if live(2):
                        act.wait_ge(probs_turned, G - 1)
                        act.wait_ge(out_mm, before(b, GROUPS, i - 2, 4))
                        act.activation(probs_h[:, (n - 2) % 4, :], ps[:, 4 + n % 2, :], ACT.Copy).then_inc(probs_high, 1)
                    if live(1):
                        act.wait_ge(shifted, G)
                        act.activation(probs[:, (n - 1) % 2, :], probs[:, (n - 1) % 2, :], ACT.Exp,
                                       scale=SCALE / QSCALE ** 2).then_inc(exp_done, 1)

                pipeline(act, attend)

                for g in range(NG):
                    for c in range(KC):
                        high_part(S_ATT + g * KC + c, c, g)
                for g in range(NG):
                    for c in range(KC):
                        high_part(S_LN2 + g * KC + c, c, g)
                with act.Fori(0, NB) as q:
                    for m in range(MF):
                        if m == 0:
                            act.wait_ge(low_done, (b + 1) * SPLITS)
                        act.wait_ge(fc1_mm, b * (NB * MF) + q * MF + (m + 1))
                        act.wait_ge(g_low, b * (NB * MF) + q * MF + max(0, m - 2))
                        act.activation(gelu[m % 3], ps[:, m % 3, 0:MB], ACT.Gelu, bias=f_bias[:, m:m + 1],
                                       scale=1 / WSCALE).then_inc(gelu_done, 1)

        @block.vector
        def _(dve):
            dve.wait_ge(silu_tr, 1)
            dve.tensor_copy(silu_t[:, 0:KF, :], ps[:, 7, 0:KF * B].rearrange("p (k b) -> p k b", b=B)).then_inc(silu_cp, 1)
            dve.tensor_copy(silu_t[0:REM, KF, :], ps[0:REM, 7, KF * B:KC * B]).then_inc(silu_cp, 1)
            dve.wait_ge(cols_tr, 1)
            dve.tensor_copy(f_bias[:, :], ps[:, 7, 64:64 + MF]).then_inc(cols_cp, 1)
            dve.wait_ge(rows_loaded, 16 * 6)
            dve.tensor_scalar(bias_h, bias_f, WSCALE, None, ALU.mult).then_inc(bias_split, 1)
            dve.wait_ge(bias_split, 1)
            dve.scalar_tensor_tensor(out=bias_l, in0=bias_f, scalar=WSCALE, in1=bias_h, op0=ALU.mult, op1=ALU.subtract).then_inc(bias_split, 1)
            dve.wait_ge(ada_mm, KC)
            dve.wait_ge(ada_b_in, 16)
            full_banks = VECTORS * D // 512
            dve.tensor_tensor(ada_out[:, 0:full_banks * 512].rearrange("b (k n) -> b k n", n=512), ps[0:B, 0:full_banks, :],
                              ada_bias[:, 0:full_banks * 512].rearrange("b (k n) -> b k n", n=512), ALU.add)
            rest = VECTORS * D - full_banks * 512
            dve.tensor_tensor(ada_out[:, full_banks * 512:], ps[0:B, full_banks, 0:rest], ada_bias[:, full_banks * 512:], ALU.add).then_inc(ada_added, 1)
            for j, (src, h, l, n, last) in enumerate(jobs):
                dve.wait_ge(w_high, j + 1)
                r = slice(0, REM if last else P)
                if j < W1_JOB:
                    for k in range(3):
                        last_write = dve.scalar_tensor_tensor(out=of_head(l[r])[:, k], in0=by_head(stage_of(j)[r])[:, k], scalar=WSCALE,
                                                              in1=of_head(h[r])[:, k], op0=ALU.mult, op1=ALU.subtract)
                    last_write.then_inc(w_low, 1)
                else:
                    dve.scalar_tensor_tensor(out=l[r], in0=stage_of(j)[r], scalar=WSCALE, in1=h[r], op0=ALU.mult, op1=ALU.subtract).then_inc(w_low, 1)

            with dve.Fori(0, B) as b:
                def normalize(g, first):
                    t0 = g % NG * 4
                    for t in range(4):
                        for k in range(2):
                            last = dve.bn_stats(stats[:, t, k, :], tok[:, t0 + t, k * HALF:(k + 1) * HALF])
                    last.then_inc(stats_done, 1)
                    dve.wait_ge(stats_done, b * (2 * NG) + g + 1)
                    passed(dve)
                    for t in range(4):
                        last = dve.bn_aggr(mv[:, t0 + t, :], stats[:, t, :, :])
                    last.then_inc(mean_done, 1)
                    dve.wait_ge(mean_done, b * (2 * NG) + g + 1)
                    dve.wait_ge(rstd_done, b * (2 * NG) + g + 1)
                    for t in range(4):
                        if t >= 2:
                            dve.wait_ge(norm_used, b * (4 * NG) + g * 2 + t - 1)
                        dve.tensor_scalar(norm[t % 2], tok[:, t0 + t, :], mv[:, t0 + t, 0:1], rstd[:, t0 + t:t0 + t + 1],
                                          ALU.subtract, ALU.mult).then_inc(norm_done, 1)

                def full_value(j, c, shift):
                    dve.wait_ge(split_mm, b * SPLITS + j + 1)
                    dve.wait_ge(low_done, before(b, SPLITS, j, 2))
                    if shift is None:
                        dve.tensor_scalar(full[j % 2], ps[:, c, :], 1.0, None, ALU.mult).then_inc(full_done, 1)
                    else:
                        dve.tensor_scalar(full[j % 2], ps[:, c, :], mod[:, (shift + 1) * KC + c:(shift + 1) * KC + c + 1],
                                          mod[:, shift * KC + c:shift * KC + c + 1], ALU.mult, ALU.add).then_inc(full_done, 1)

                dve.wait_ge(mod_tr, b + 1)
                dve.tensor_copy(mod[:, :], ps[:, 7, 0:VECTORS * KC]).then_inc(mod_cp, 1)
                dve.wait_ge(mod_cp, b * 4 + 1)
                dve.wait_ge(gates_in, (b + 1) * 32)
                for v in (SCALE_MSA, SCALE_MLP):
                    dve.tensor_scalar(mod[:, v * KC:(v + 1) * KC], mod[:, v * KC:(v + 1) * KC], 1.0, None, ALU.add).then_inc(mod_cp, 1)
                dve.tensor_scalar(gates[:, :, :], gates[:, :, :], 1 / WSCALE, None, ALU.mult).then_inc(mod_cp, 1)
                dve.wait_ge(mod_cp, (b + 1) * 4)
                dve.wait_ge(x_in, (b + 1) * (E * 16))
                for g in range(NG):
                    normalize(g, True)
                    for c in range(KC):
                        full_value(S_LN1 + g * KC + c, c, SHIFT_MSA)
                with dve.Fori(0, NT // 2) as i:
                    for u in range(2):
                        for k in range(2):
                            dve.wait_ge(qkv_high, b * (2 * NT) + i * 4 + (u * 2 + k + 1))
                            for bank in (2 * k, 2 * k + 1):
                                h, qkv = in_bank(u, bank)
                                dst = qkv_tok[:, u, h, :]
                                for part, (low, high) in enumerate(((QL, QL + DH), (KH + 2 * DH, KH), (VL, VH))):
                                    last = dve.scalar_tensor_tensor(out=dst[:, :, low:low + DH], in0=qkv[:, :, part], scalar=QSCALE / WSCALE,
                                                                    in1=dst[:, :, high:high + DH], op0=ALU.mult, op1=ALU.subtract)
                            last.then_inc(qkv_done, 1)
                for u in range(2):
                    dve.wait_ge(qkv_stored[u], (b + 1) * (NT // 2 * 16))
                passed(dve)

                def attend(i, n, live):
                    G = b * GROUPS + i
                    s1, s2, s4 = (n - 1) % 2, n % 2, n % 2
                    scores = ps[:, 2 + s1, :].rearrange("p (k c) -> p k c", k=4)
                    outputs = ps[:, 6 + s4, 0:4 * (DH + 1)].rearrange("p (k c) -> p k c", k=4)
                    if live(1):
                        dve.wait_ge(scores_mm, G)
                        dve.tensor_reduce(negmax[:, s1, :], scores, AX.X, ALU.max, negate=True).then_inc(max_done, 1)
                    if live(4):
                        dve.wait_ge(out_mm, G - 3)
                        dve.reciprocal(inv_sum[:, s4, :], outputs[:, :, DH]).then_inc(inv_done, 1)
                    if live(1):
                        dve.wait_ge(max_done, G)
                        dve.wait_ge(probs_turned, before(b, GROUPS, i - 1, 2))
                        dve.tensor_tensor(probs[:, s1, :].rearrange("p (k c) -> p k c", k=4), scores,
                                          negmax[:, s1, :].unsqueeze(2).broadcast_to([P, 4, P]), ALU.add).then_inc(shifted, 1)
                    if live(4):
                        dve.wait_ge(inv_done, G - 3)
                        dve.tensor_tensor(tok_f[:, bass.ds((i - 4) * (4 * DH), 4 * DH)].rearrange("p (k c) -> p k c", k=4),
                                          outputs[:, :, 0:DH], inv_sum[:, s4, :].unsqueeze(2).broadcast_to([P, 4, DH]), ALU.mult).then_inc(out_done, 1)
                    if live(2):
                        dve.wait_ge(probs_high, G - 1)
                        dve.wait_ge(out_mm, before(b, GROUPS, i - 2, 4))
                        slot = (n - 2) % 4
                        dve.tensor_tensor(probs_l[:, slot, :], ps[:, 4 + s2, :], probs_h[:, slot, :], ALU.subtract).then_inc(probs_low, 1)

                pipeline(dve, attend)

                for g in range(NG):
                    for c in range(KC):
                        full_value(S_ATT + g * KC + c, c, None)
                with dve.Fori(0, NT // 2) as i:
                    for u in range(2):
                        t = i * 2 + u
                        row = tok[:, bass.ds(t, 1), :].rearrange("p t (k n) -> p (t k) n", k=2)
                        dve.wait_ge(proj_mm, b * NT + t + 1)
                        dve.wait_ge(xres_in, (b + 1) * (E * 16))
                        dve.tensor_tensor(row, ps[:, 4 + 2 * u:6 + 2 * u, 0:HALF],
                                          gates[:, 0, :].rearrange("p (k n) -> p k n", k=2), ALU.mult).then_inc(proj_gated, 1)
                        dve.wait_ge(proj_gated, b * NT + t + 1)
                        row, res = (a[:, bass.ds(t, 1), :].rearrange("p t d -> p (t d)") for a in (tok, x_res))
                        dve.tensor_tensor(row, row, res, ALU.add).then_inc(x1_done, 1)
                dve.wait_ge(x1_done, (b + 1) * NT)
                for g in range(NG):
                    normalize(NG + g, False)
                    for c in range(KC):
                        full_value(S_LN2 + g * KC + c, c, SHIFT_MLP)
                with dve.Fori(0, NB) as q:
                    for m in range(MF):
                        M = b * (NB * MF) + q * MF + (m + 1)
                        dve.wait_ge(gelu_done, M)
                        if m == 0:
                            dve.wait_ge(fc2_mm, b * NT + q * 2)
                        dve.tensor_copy(gh[:, m, :], gelu[m % 3]).then_inc(g_high, 1)
                        dve.wait_ge(g_high, M)
                        dve.tensor_tensor(gl[:, m, :], gelu[m % 3], gh[:, m, :], ALU.subtract).then_inc(g_low, 1)
                    for u in range(2):
                        t = q * 2 + u
                        dve.wait_ge(fc2_mm, b * NT + t + 1)
                        dve.tensor_tensor(norm[u].rearrange("p (k n) -> p k n", k=2), ps[:, 4 + 2 * u:6 + 2 * u, 0:HALF],
                                          gates[:, 1, :].rearrange("p (k n) -> p k n", k=2), ALU.mult).then_inc(mlp_gated, 1)
                        dve.wait_ge(mlp_gated, b * NT + t + 1)
                        row = tok[:, bass.ds(t, 1), :].rearrange("p t d -> p (t d)")
                        dve.tensor_tensor(row, row, norm[u], ALU.add).then_inc(x2_done, 1)

        @block.tensor
        def _(pe):
            pe.wait_ge(silu_done, 1)
            pe.wait_ge(consts_set, IDENT_SET)
            for k in range(KC):
                n = min(P, D - k * P)
                last = pe.transpose(ps[0:n, 7, k * B:(k + 1) * B], silu_c[:, k * P:k * P + n], ident[0:B, 0:B])
            last.then_inc(silu_tr, 1)
            pe.wait_ge(silu_cp, 2)
            pe.wait_ge(rows_loaded, 16 * 6)
            pe.transpose(ps[:, 7, 64:64 + MF], col_rows, ident[0:MF, 0:MF]).then_inc(cols_tr, 1)
            for k in range(KC):
                rows = min(P, D - k * P)
                pe.wait_ge(ada_w_in[k % 3], 16 * (k // 3 + 1))
                for n in range(0, VECTORS * D, 512):
                    w = min(512, VECTORS * D - n)
                    last = pe.matmul(ps[0:B, n // 512, 0:w], silu_t[0:rows, k, :], ada_stage[k % 3][0:rows, n:n + w],
                                     start=(k == 0), stop=(k == KC - 1))
                last.then_inc(ada_mm, 1)
            pe.wait_ge(cols_cp, 1)
            pe.wait_ge(ada_added, 1)
            pe.wait_ge(w_low, len(jobs))
            pe.wait_ge(bias_in, 16 * 6)
            pe.wait_ge(consts_set, CONSTANTS_SET)

            def passes(wh, wl):
                for c in range(KC):
                    yield xh[:, c, :], wh[:, c, :]
                for c in range(KC):
                    yield xh[:, c, :], wl[:, c, :]
                for c in range(KF):
                    yield xl[:, c, :], wh[:, c, :]

            def tokens(t):
                return slice(t * P, (t + 1) * P) if isinstance(t, int) else bass.ds(t * P, P)

            def by_tokens(t, bank, wh, wl, col, n, bias, done):
                for i, (xa, wa) in enumerate(passes(wh, wl)):
                    for k in range(2):
                        pe.matmul(ps[:, bank + k, 0:n], xa[:, tokens(t)], wa[:, col + k * n:col + (k + 1) * n],
                                  start=(i == 0), stop=False)
                for k in range(2):
                    last = pe.matmul(ps[:, bank + k, 0:n], pick[:, bias, :], bias_rows[:, col + k * n:col + (k + 1) * n],
                                     start=False, stop=True)
                last.then_inc(done, 1)

            with pe.Fori(0, B) as b:
                def turn(g, j0, normalized):
                    t0 = g % NG * 4
                    if g % NG:
                        pe.wait_ge(full_done, b * SPLITS + j0)
                    for t in range(4):
                        if normalized:
                            pe.wait_ge(norm_done, b * (2 * NT) + g * 4 + t + 1)
                        src = norm[t % 2] if normalized else tok[:, t0 + t, :]
                        at = slice(t * P, (t + 1) * P)
                        for c in range(KF):
                            last = pe.transpose(ps[:, c, at], src[:, c * P:(c + 1) * P], ident[:, :])
                            if t == 3:
                                last.then_inc(split_mm, 1)
                        pe.transpose(ps[:, KF, at], src[:, D - P:D], ident[:, :])
                        last = pe.transpose(ps[0:REM, KF, at], src[:, KF * P:D], ident[:, :])
                        if t == 3:
                            last.then_inc(split_mm, 1)
                        if normalized and t < 2:
                            last.then_inc(norm_used, 1)

                pe.wait_ge(mod_in, (b + 1) * 16)
                pe.wait_ge(x2_done, b * NT)
                passed(pe)
                pe.transpose(ps[:, 7, 0:VECTORS * KC], mod_rows, ident[0:VECTORS * KC, 0:VECTORS * KC]).then_inc(mod_tr, 1)
                for g in range(NG):
                    turn(g, S_LN1 + g * KC, True)

                pe.wait_ge(low_done, b * SPLITS + S_ATT)
                passed(pe)
                for t in range(2):
                    for k in range(2):
                        by_tokens(t, 4 * t + 2 * k, wq_h, wq_l, k * 2 * QC, QC, 0, qkv_mm[k])
                with pe.Fori(1, NT // 2) as i:
                    for u in range(2):
                        for k in range(2):
                            pe.wait_ge(qkv_done, b * (2 * NT) + i * 4 + (2 * u + k - 3))
                            by_tokens(i * 2 + u, 4 * u + 2 * k, wq_h, wq_l, k * 2 * QC, QC, 0, qkv_mm[k])
                pe.wait_ge(qkv_done, (b + 1) * (2 * NT))
                pe.wait_ge(ones_set, b + 1)
                passed(pe)

                def attend(i, n, live):
                    G = b * GROUPS + i
                    if live(1):
                        s = (n - 1) % 2
                        pe.wait_ge(qk_copied, G)
                        pe.wait_ge(shifted, before(b, GROUPS, i - 1, 2))
                        pe.matmul(ps[:, 2 + s, :].rearrange("p (k c) -> p k c", k=4), own[:, :],
                                  others[:, :].unsqueeze(1).broadcast_to([P, 4, P]), start=True, stop=False)
                        for k in range(4):
                            last = pe.matmul(ps[:, 2 + s, k * P:(k + 1) * P], qk_t[0:3 * DH, s, 0, k * P:(k + 1) * P],
                                             qk_t[0:3 * DH, s, 1, k * P:(k + 1) * P], start=False, stop=(k == 3))
                        last.then_inc(scores_mm, 1)
                    if live(0):
                        pe.wait_ge(heads_in[n // 2], b * (GROUPS // RING * 16) + (i - n) * 2 + 16)
                        pe.wait_ge(qk_copied, before(b, GROUPS, i, 2))
                        passed(pe)
                        for half, at in enumerate((QL, KH)):
                            for k in range(4):
                                last = pe.transpose(ps_half[0:3 * DH, n % 2, (half * 4 + k) * P:(half * 4 + k + 1) * P],
                                                    qkv_head[:, n, k, at:at + 3 * DH], ident_h[:, :])
                        last.then_inc(qk_turned, 1)
                    if live(4):
                        s = n % 2
                        pe.wait_ge(probs_low, G - 3)
                        pe.wait_ge(out_done, before(b, GROUPS, i - 4, 2))
                        for k in range(4):
                            at, o = slice(k * P, (k + 1) * P), k * (DH + 1)
                            v = qkv_head[:, (n - 4) % RING, k, :]
                            pe.matmul(ps[:, 6 + s, o:o + DH + 1], probs_h[:, n % 4, at], v[:, VH:VH + DH + 1], start=True, stop=False)
                            pe.matmul(ps[:, 6 + s, o:o + DH], probs_h[:, n % 4, at], v[:, VL:VL + DH], start=False, stop=False)
                            last = pe.matmul(ps[:, 6 + s, o:o + DH + 1], probs_l[:, n % 4, at], v[:, VH:VH + DH + 1], start=False, stop=True)
                        last.then_inc(out_mm, 1)
                    if live(2):
                        s = n % 2
                        pe.wait_ge(exp_done, G - 1)
                        pe.wait_ge(probs_low, before(b, GROUPS, i - 2, 2))
                        for k in range(4):
                            last = pe.transpose(ps[:, 4 + s, k * P:(k + 1) * P], probs[:, s, k * P:(k + 1) * P], ident[:, :])
                        last.then_inc(probs_turned, 1)

                pipeline(pe, attend)

                pe.wait_ge(out_done, (b + 1) * GROUPS)
                for g in range(NG):
                    turn(g, S_ATT + g * KC, False)
                pe.wait_ge(low_done, b * SPLITS + S_LN2)
                passed(pe)
                with pe.Fori(0, NT // 2) as i:
                    for u in range(2):
                        pe.wait_ge(proj_gated, b * NT + i * 2)
                        by_tokens(i * 2 + u, 4 + 2 * u, wp_h, wp_l, 0, HALF, 1, proj_mm)
                for g in range(NG):
                    turn(NG + g, S_LN2 + g * KC, True)

                pe.wait_ge(low_done, (b + 1) * SPLITS)
                pe.wait_ge(proj_gated, (b + 1) * NT)
                passed(pe)
                with pe.Fori(0, NB) as q:
                    for m in range(MF):
                        pe.wait_ge(gelu_done, b * (NB * MF) + q * MF + max(0, m - 2))
                        ops = list(passes(w1_h, w1_l))
                        for i, (xa, wa) in enumerate(ops):
                            last = pe.matmul(ps[:, m % 3, 0:MB], wa[:, m * P:(m + 1) * P], xa[:, bass.ds(q * MB, MB)],
                                             start=(i == 0), stop=(i == len(ops) - 1))
                        last.then_inc(fc1_mm, 1)
                    for u in range(2):
                        pe.wait_ge(mlp_gated, b * NT + q * 2)
                        at = slice(u * P, (u + 1) * P)
                        for m in range(MF):
                            if u == 0:
                                pe.wait_ge(g_low, b * (NB * MF) + q * MF + (m + 1))
                            for i, (ga, wa) in enumerate(((gh, w2_h), (gh, w2_l), (gl, w2_h))):
                                for k in range(2):
                                    pe.matmul(ps[:, 4 + 2 * u + k, 0:HALF], ga[:, m, at], wa[:, m, k * HALF:(k + 1) * HALF],
                                              start=(m == 0 and i == 0), stop=False)
                        for k in range(2):
                            last = pe.matmul(ps[:, 4 + 2 * u + k, 0:HALF], pick[:, 2, :], bias_rows[:, k * HALF:(k + 1) * HALF],
                                             start=False, stop=True)
                        last.then_inc(fc2_mm, 1)


_INS = ['x', 'cond_1152', 'L0_cond_qkv_w', 'L0_cond_qkv_b', 'L0_cond_proj_w', 'L0_cond_proj_b', 'L0_cond_fc1_w',
        'L0_cond_fc1_b', 'L0_cond_fc2_w', 'L0_cond_fc2_b', 'L0_cond_ada_w', 'L0_cond_ada_b']
_OUTS = [((8, 1024, 576), 'float32')]


def kernel(**inputs):
    import numpy as _np
    import concourse.bacc as _bacc
    from concourse import mybir as _mybir
    from concourse.bass_utils import run_bass_kernel_spmd as _run

    nc = _bacc.Bacc("TRN2", target_bir_lowering=False, num_devices=1)
    arrays, args = {}, []
    for name in _INS:
        a = _np.ascontiguousarray(inputs[name])
        arrays[f"in_{name}_dram"] = a
        args.append(nc.dram_tensor(f"in_{name}_dram", a.shape, _mybir.dt.from_np(a.dtype), kind="ExternalInput").ap())
    for i, (shape, dtype) in enumerate(_OUTS):
        dt = _mybir.dt.from_np(_np.dtype(dtype))
        args.append(nc.dram_tensor(f"out_{i}_dram", shape, dt, kind="ExternalOutput").ap())
    block_kernel(nc, *args)
    r = _run(nc, [arrays], core_ids=[0])
    got = tuple(r.results[0][f"out_{i}_dram"] for i in range(len(_OUTS)))
    return got[0]
```

```python
from contextlib import ExitStack

import concourse.bass as bass
from concourse import mybir

F32 = mybir.dt.float32
F16 = mybir.dt.float16
BF16 = mybir.dt.bfloat16
ALU = mybir.AluOpType
ACT = mybir.ActivationFunctionType
AX = mybir.AxisListType

P = 128
HEADS = 16
EPS = 1e-6
WSCALE = 256.0
QSCALE = 16.0
OFF = -1e30
RING = 8
LAGS = 5
VECTORS = 6
SHIFT_MSA, SCALE_MSA, GATE_MSA, SHIFT_MLP, SCALE_MLP, GATE_MLP = range(VECTORS)
STAGES = 6
IDENT_SET, BIAS_SET, CONSTANTS_SET = 2, 5, 18


def block_kernel(nc, x, cond, qkv_w, qkv_b, proj_w, proj_b, fc1_w, fc1_b, fc2_w, fc2_b, ada_w, ada_b, out):
    B, T, D = x.shape
    DH = D // HEADS
    MLP = fc1_w.shape[1]
    NT = T // P
    NG = NT // 4
    KC = -(-D // P)
    KF = D // P
    REM = D - KF * P
    MF = MLP // P
    HALF = D // 2
    MB = 256
    NB = T // MB
    SCALE = DH ** -0.5
    E = P // HEADS
    NBLK = T // E
    GROUPS = NBLK // 4
    QL, KH, VL, VH = 0, 3 * DH, 6 * DH, 7 * DH
    HC = 8 * DH
    HP = HC + 2
    TB = P // E
    QC = 3 * D // 4
    SPLITS = NG * KC * 3
    S_LN1, S_ATT, S_LN2 = 0, NG * KC, 2 * NG * KC
    LATE_AT = 3
    NEXT_AT = 11
    UNSHIFTED = 2 * NG * KC
    assert REM == 64 and MF % 3 == 0 and SPLITS % 2 == 0 and NBLK == P and E == NT and GROUPS % RING == 0

    with ExitStack() as ctx:
        def sb(name, shape, dt):
            return ctx.enter_context(nc.sbuf_tensor(name, shape, dt))

        def sem(name):
            return ctx.enter_context(nc.semaphore(name))

        qkv_dram = nc.dram_tensor("qkv", (T, HEADS * HC), F16).ap()
        gates_dram = nc.dram_tensor("gates_rows", (B, 2, D), F32).ap()

        wq_h, wq_l = sb("wq_h", [P, KC, 3 * D], F16), sb("wq_l", [P, KC, 3 * D], F16)
        wp_h, wp_l = sb("wp_h", [P, KC, D], F16), sb("wp_l", [P, KC, D], F16)
        w1_h, w1_l = sb("w1_h", [P, KC, MLP], F16), sb("w1_l", [P, KC, MLP], F16)
        w2_h, w2_l = sb("w2_h", [P, MF, D], F16), sb("w2_l", [P, MF, D], F16)

        tok = sb("tok", [P, NT, D], F32)
        xr = sb("xr", [P, (2 * KC - 1) * T], F16)
        xh = xr[:, 0:KC * T].rearrange("p (c t) -> p c t", c=KC)
        xl = xr[:, KC * T:].rearrange("p (c t) -> p c t", c=KC - 1)
        qk_t = xr[:, 0:2048].rearrange("p (s k t) -> p s k t", s=2, k=2)
        probs = xr[:, 2048:4096].bitcast(F32).rearrange("p (s t) -> p s t", s=2)
        vr = sb("vr", [P, 2 * NT * D + 6 * MB], F16)
        vr32 = vr[:, :].bitcast(F32)
        qkv_tok = tok[:, :, :].rearrange("p t d -> p (t d)").bitcast(F16).rearrange("p (s h c) -> p s h c", s=2, c=HC)
        qkv_head = vr[:, 0:RING * 4 * HP].rearrange("p (s k c) -> p s k c", s=RING, k=4)
        xn = vr32[:, 0:NT * D].rearrange("p (i d) -> p i d", i=NT)
        gelu_parts = vr[:, 2 * NT * D:].rearrange("p (k m t) -> p k m t", k=2, m=3)
        gh, gl = gelu_parts[:, 0], gelu_parts[:, 1]
        work = sb("work", [P, 3 * 512 + 3 * MB], F32)
        turned = work[:, 0:2048].bitcast(F16).rearrange("p (k s t) -> p k s t", k=2, s=4)
        probs_h, probs_l = turned[:, 0], turned[:, 1]
        low32 = [work[:, 512 * j:512 * j + 512] for j in range(3)]
        gelu = [work[:, 1536 + MB * j:1536 + MB * j + MB] for j in range(3)]
        gated = [work[:, D * j:D * j + D] for j in range(2)]
        gates = sb("gates", [P, 2, D], F32)
        mods = sb("mods", [P, B, VECTORS * KC], F32)
        mod = sb("mod", [P, 1, VECTORS * KC], F32)
        stats = sb("stats", [P, NT, 2, 6], F32)
        mv = sb("mv", [P, NT, 2], F32)
        rstd = sb("rstd", [P, NT], F32)
        negmax = sb("negmax", [P, 2, 4], F32)
        inv_sum = sb("inv_sum", [P, 2, 4], F32)

        ident = sb("ident", [P, P], F32)
        ident_h = sb("ident_h", [P, P], F16)
        xb = sb("xb", [P, T], F16)
        pick = sb("pick", [P, P], F16)
        bias_rows = sb("bias_rows", [P, D], F16)
        own = sb("own", [P, P], BF16)
        others = sb("others", [P, P], BF16)
        f_bias = sb("f_bias", [P, MF], F32)
        minus_half = sb("minus_half", [P, 4], F32)
        epsilon = sb("epsilon", [P, 4], F32)
        silu_t = sb("silu_t", [P, KC, B], F32)
        ps = ctx.enter_context(nc.psum_tensor("ps", [P, 8, 512], F32))
        ps_half = ps[:, :, :].rearrange("p k n -> p (k n)").bitcast(F16).rearrange("p (k n) -> p k n", k=8)

        tok_f = tok[:, :, :].rearrange("p t d -> p (t d)")
        xr_f = xr[:, :].bitcast(F32)
        ada_stage = [tok_f[:, 0:VECTORS * D], vr32[:, 0:VECTORS * D], xr_f[:, 0:VECTORS * D]]
        w_stage = [r[:, n * MLP:n * MLP + MLP] for r in (tok_f, vr32, xr_f) for n in range(2)]
        ada_bias = w1_h[:, :, :].rearrange("p c n -> p (c n)").bitcast(F32)[0:B, 0:VECTORS * D]
        ada_out = w1_l[:, :, :].rearrange("p c n -> p (c n)").bitcast(F32)[0:B, 0:VECTORS * D]
        w2_f = w2_h[:, :, :].rearrange("p c n -> p (c n)")
        bias_f = w2_f[0:1, 0:10 * D].bitcast(F32)
        bias_h = w2_f[0:1, 10 * D:15 * D]
        w2l_h = w2_l[:, :, :].rearrange("p c n -> p (c n)")
        bias_l = w2l_h[0:1, 10 * D:15 * D]
        w2l_f = w2_l[:, :, :].rearrange("p c n -> p (c n)").bitcast(F32)
        cond_in, silu_c = w2l_f[0:B, 0:D], w2l_f[0:B, D:2 * D]
        col_rows = w2l_f[0:MF, 2 * D:2 * D + P]

        consts_set, cond_in_s, ada_b_in = (sem(n) for n in ("consts_set", "cond_in_s", "ada_b_in"))
        ada_w_in = [sem(f"ada_w_in{i}") for i in range(3)]
        rows_loaded, silu_done, silu_tr, silu_cp = (sem(n) for n in ("rows_loaded", "silu_done", "silu_tr", "silu_cp"))
        ada_mm, ada_added, gates_scaled, gates_stored, mods_tr, mods_set, bias_split, bias_in = (
            sem(n) for n in ("ada_mm", "ada_added", "gates_scaled", "gates_stored", "mods_tr", "mods_set", "bias_split", "bias_in"))
        cols_tr, cols_cp = sem("cols_tr"), sem("cols_cp")
        w_in = [sem(f"w_in{i}") for i in range(STAGES)]
        w_high, w_low = sem("w_high"), sem("w_low")
        waits_passed = sem("waits_passed")
        x_in, gates_in, mod_cp = (sem(n) for n in ("x_in", "gates_in", "mod_cp"))
        stats_done, mean_done, eps_done, rstd_done, norm_done = (
            sem(n) for n in ("stats_done", "mean_done", "eps_done", "rstd_done", "norm_done"))
        split_mm, high_done, unshifted, low_done = (sem(n) for n in ("split_mm", "high_done", "unshifted", "low_done"))
        qkv_mm = [sem("qkv_mm0"), sem("qkv_mm1")]
        qkv_high, qkv_done = sem("qkv_high"), sem("qkv_done")
        qkv_stored = [sem("qkv_stored0"), sem("qkv_stored1")]
        ones_set = sem("ones_set")
        heads_in = [sem(f"heads_in{i}") for i in range(RING // 2)]
        qk_turned, qk_copied, scores_mm, max_done, shifted, exp_done = (
            sem(n) for n in ("qk_turned", "qk_copied", "scores_mm", "max_done", "shifted", "exp_done"))
        probs_turned, probs_high, probs_low, out_mm, inv_done, out_done = (
            sem(n) for n in ("probs_turned", "probs_high", "probs_low", "out_mm", "inv_done", "out_done"))
        xres_in = sem("xres_in")
        proj_mm, proj_gated, x1_done = (sem(n) for n in ("proj_mm", "proj_gated", "x1_done"))
        fc1_mm, gelu_done, g_high, g_low, g_used, fc2_mm, mlp_gated, x2_done, stored = (
            sem(n) for n in ("fc1_mm", "gelu_done", "g_high", "g_low", "g_used", "fc2_mm", "mlp_gated", "x2_done", "stored"))

        jobs = []
        for w, h, l, n in ((qkv_w, wq_h, wq_l, 3 * D), (fc1_w, w1_h, w1_l, MLP)):
            for c in range(KF):
                jobs.append((w[c * P:(c + 1) * P, :], h[:, c, :], l[:, c, :], n, False))
            jobs.append((w[KF * P:D, :], h[:, KF, :], l[:, KF, :], n, True))
        jobs.append((proj_w[0:KF * P, :].rearrange("(c p) n -> p c n", p=P), wp_h[:, 0:KF, :], wp_l[:, 0:KF, :], KF * D, False))
        jobs.append((proj_w[KF * P:D, :], wp_h[:, KF, :], wp_l[:, KF, :], D, True))
        for c in range(0, MF, 4):
            k = min(4, MF - c)
            jobs.append((fc2_w[c * P:(c + k) * P, :].rearrange("(c p) n -> p c n", p=P), w2_h[:, c:c + k, :], w2_l[:, c:c + k, :], k * D, False))
        W1_JOB, W2_JOB = KC, 2 * KC + 2

        def stage_of(j):
            _, h, _, n, _ = jobs[j]
            s = w_stage[j % STAGES][:, 0:n]
            return s if len(h.shape) == 2 else s.rearrange("p (c n) -> p c n", n=D)

        by_head = lambda a: a.rearrange("p (k h d) -> p k h d", k=3, d=DH)
        of_head = lambda a: a.rearrange("p (h k d) -> p k h d", k=3, d=DH)

        block = ctx.enter_context(nc.Block())

        def before(b, per, j, ring):
            return b * per + (max(0, j - ring + 1) if isinstance(j, int) else j - (ring - 1))

        def pipeline(engine, body):
            for i in range(RING):
                body(i, i, lambda lag: i >= lag)
            with engine.Fori(0, GROUPS // RING - 1) as r:
                for n in range(RING):
                    body(r * RING + (RING + n), n, lambda lag: True)
            for i in range(GROUPS, GROUPS + LAGS):
                body(i, i % RING, lambda lag: i - lag < GROUPS)

        def passed(engine):
            engine.sem_inc(waits_passed, 1)

        def split_place(b, j):
            c, n = j % KC, j // KC % NG
            shift = {S_LN1: SHIFT_MSA, S_ATT: None, S_LN2: SHIFT_MLP}[j // (NG * KC) * (NG * KC)]
            vectors = None if shift is None else [mod[:, 0, v * KC + c:v * KC + c + 1] for v in (shift, shift + 1)]
            if j < S_LN1 + KC and isinstance(b, int) and b == 0:
                bank = c
            elif j < S_LN1 + KC or j >= S_LN2 + KC:
                bank = 4
            elif j < S_ATT:
                bank = 4 + c % 4
            else:
                bank = 0 if j == S_LN2 + KF else c
            return c, bank, slice(n * 512, (n + 1) * 512), vectors

        def unshifted_before(j):
            return j if j < S_ATT else j - NG * KC

        def proj_bank(t):
            return 6 if t % 2 == 0 else 4

        def fc1_bank(m):
            return 5 + (m + 1) % 3

        def in_bank(u, bank):
            return slice(4 * bank, 4 * bank + 4), ps[:, 4 * u + bank, 0:QC].rearrange("p (h k d) -> p h k d", k=3, d=DH)

        @block.sync
        def _(sp):
            sp.dma_start(cond_in, cond).then_inc(cond_in_s, 16)
            sp.dma_start(ada_bias, ada_b.rearrange("(a n) -> a n", a=1).broadcast_to([B, VECTORS * D])).then_inc(ada_b_in, 16)
            sp.dma_start(col_rows, fc1_b.rearrange("(m p) -> m p", p=P)).then_inc(rows_loaded, 16)
            for k in range(3):
                sp.dma_start(of_head(bias_f[:, 0:3 * D])[:, k], by_head(qkv_b.rearrange("(a n) -> a n", a=1))[:, k]).then_inc(rows_loaded, 16)
            for i, v in enumerate((proj_b, fc2_b)):
                sp.dma_start(bias_f[:, (3 + i) * D:(4 + i) * D], v.rearrange("(a n) -> a n", a=1)).then_inc(rows_loaded, 16)
            for k in range(KC):
                rows = min(P, D - k * P)
                if k >= 3:
                    sp.wait_ge(ada_mm, k - 2)
                sp.dma_start(ada_stage[k % 3][0:rows, :], ada_w[k * P:k * P + rows, :]).then_inc(ada_w_in[k % 3], 16)
            sp.wait_ge(consts_set, BIAS_SET)
            sp.wait_ge(bias_split, 2)
            for dst, row, at, n in ((wq_l[:, KF, :], REM, 0, 3 * D), (wp_l[:, KF, :], REM, 3 * D, D), (bias_rows, 0, 4 * D, D)):
                sp.dma_start(dst[row:row + 1, 0:n], bias_h[:, at:at + n]).then_inc(bias_in, 16)
                sp.dma_start(dst[row + 1:row + 2, 0:n], bias_l[:, at:at + n]).then_inc(bias_in, 16)
            sp.wait_ge(gates_scaled, 2)
            ada_v = ada_out.rearrange("b (v d) -> b v d", v=VECTORS)
            for i, v in enumerate((GATE_MSA, GATE_MLP)):
                sp.dma_start(gates_dram[:, i, :], ada_v[:, v, :]).then_inc(gates_stored, 16)
            sp.wait_ge(ada_mm, KC)
            sp.wait_ge(gates_stored, 32)
            sp.wait_ge(mods_tr, 1)
            sp.wait_ge(bias_in, 16 * 6)
            sp.wait_ge(cols_tr, 1)
            for j, (src, h, l, n, last) in enumerate(jobs):
                if j >= STAGES:
                    sp.wait_ge(w_low, j - STAGES + 1)
                dst = stage_of(j)
                if last:
                    sp.dma_start(dst[0:REM], src).then_inc(w_in[j % STAGES], 16)
                    sp.dma_start(dst[REM:P], src).then_inc(w_in[j % STAGES], 16)
                else:
                    sp.dma_start(dst[0:REM], src[0:REM]).then_inc(w_in[j % STAGES], 16)
                    sp.dma_start(dst[REM:P], src[REM:P]).then_inc(w_in[j % STAGES], 16)
            sp.wait_ge(w_low, len(jobs))

            def load_x(row):
                tiles = x[row] if isinstance(row, int) else x[bass.ds(row, 1), :, :].rearrange("b n d -> (b n) d")
                tiles = tiles.rearrange("(e t j) d -> e j t d", e=E, j=TB)
                for e in range(E):
                    sp.dma_start(xn[e:P:E, :, :], tiles[e]).then_inc(x_in, 16)

            load_x(0)

            def row(b, more):
                sp.wait_ge(x2_done, b * NT)
                passed(sp)
                for i in range(2):
                    src = gates_dram[b:b + 1, i, :] if isinstance(b, int) else gates_dram[bass.ds(b, 1), i, :]
                    sp.dma_start(gates[:, i, :], src.broadcast_to([P, D])).then_inc(gates_in, 16)

                def store_qkv(t, u):
                    sp.wait_ge(qkv_done, b * (2 * NT) + t * 2 + 2)
                    sp.dma_start(qkv_dram[t * P:(t + 1) * P, :] if isinstance(t, int) else qkv_dram[bass.ds(t * P, P), :],
                                 qkv_tok[:, u, :, :].rearrange("p h c -> p (h c)")).then_inc(qkv_stored[u], 16)

                by_head_e = qkv_dram.rearrange("(t j e) (h c) -> (e h) t j c", e=E, j=TB, c=HC)

                def load_heads(t, s):
                    src = by_head_e[:, bass.ds(t, 1), s % 2 * 8:s % 2 * 8 + 8, :].rearrange("p t j c -> p (t j) c")
                    dst = qkv_head[:, 2 * s:2 * s + 2, :, 0:HC].rearrange("p s k c -> p (s k) c")
                    sp.dma_start(dst, src).then_inc(heads_in[s], 16)

                store_qkv(0, 0)
                store_qkv(1, 1)
                for t in range(2):
                    sp.wait_ge(qkv_stored[t], b * (NT // 2 * 16) + 16)
                    for s in (2 * t, 2 * t + 1):
                        load_heads(t, s)
                    store_qkv(2 + t, t)
                with sp.Fori(2, NT // 2) as i:
                    for u in range(2):
                        store_qkv(i * 2 + u, u)
                for u in range(2):
                    sp.wait_ge(qkv_stored[u], (b + 1) * (NT // 2 * 16))
                passed(sp)
                with sp.Fori(0, GROUPS // RING - 1) as r:
                    for s in range(RING // 2):
                        sp.wait_ge(out_mm, b * GROUPS + r * RING + (2 * s + 2))
                        load_heads(r * 2 + (2 + s // 2), s)

                x_rows = x[bass.ds(b, 1), :, :].rearrange("b (h e i) d -> e h (b i) d", e=E, i=NT)
                sp.wait_ge(out_mm, (b + 1) * GROUPS)
                for e in range(E):
                    sp.dma_start(xn[e * HEADS:(e + 1) * HEADS], x_rows[e]).then_inc(xres_in, 16)

                out_rows = out[bass.ds(b, 1), :, :].rearrange("b (h e i) d -> e h (b i) d", e=E, i=NT)
                if more:
                    sp.wait_ge(split_mm, (b + 1) * SPLITS)
                    load_x(b + 1)
                passed(sp)
                with sp.Fori(0, NB) as q:
                    sp.wait_ge(x2_done, b * NT + q * 2 + 2)
                    for e in range(E):
                        sp.dma_start(out_rows[e][:, bass.ds(q * 2, 2), :],
                                     tok[e * HEADS:(e + 1) * HEADS, bass.ds(q * 2, 2), :]).then_inc(stored, 16)
            with sp.Fori(0, B - 1) as b:
                row(b, True)
            row(B - 1, False)
            sp.wait_ge(stored, B * (NB * E * 16))

        @block.gpsimd
        def _(pool):
            def constant(write, n):
                write.then_inc(consts_set, 1)
                pool.wait_ge(consts_set, n)

            constant(pool.memset(ident[:, :], 0.0), 1)
            constant(pool.affine_select(out=ident[:, :], in_=ident[:, :], compare_op=ALU.not_equal, fill=1.0, base=0,
                                        pattern=[[-1, P]], channel_multiplier=1), IDENT_SET)
            constant(pool.memset(bias_rows[:, :], 0.0), 3)
            constant(pool.memset(wq_l[REM:P, KF, :], 0.0), 4)
            constant(pool.memset(wp_l[REM:P, KF, :], 0.0), BIAS_SET)
            constant(pool.memset(minus_half[:, :], -0.5), 6)
            constant(pool.memset(epsilon[:, :], EPS), 7)
            constant(pool.memset(own[:, :], 0.0), 8)
            constant(pool.affine_select(out=own[:, :], in_=own[:, :], compare_op=ALU.not_equal, fill=1.0, base=0,
                                        pattern=[[-1, E], [0, HEADS]], channel_multiplier=1), 9)
            constant(pool.memset(pick[:, :], 0.0), 10)
            constant(pool.memset(pick[0:2, :], 1.0), 11)
            constant(pool.memset(xb[REM:P, :], 0.0), 12)
            constant(pool.memset(xb[REM:REM + 2, :], 1.0), 13)
            constant(pool.memset(others[:, :], 0.0), 14)
            constant(pool.memset(others[0:E, :], OFF), 15)
            constant(pool.affine_select(out=others[0:E, :], in_=others[0:E, :], compare_op=ALU.not_equal, fill=0.0, base=0,
                                        pattern=[[-1, E], [0, HEADS]], channel_multiplier=1), 16)
            constant(pool.tensor_copy(ident_h[:, :], ident[:, :]), 17)
            pool.wait_ge(gates_stored, 32)
            pool.wait_ge(mods_tr, 1)
            constant(pool.memset(w1_l[REM:P, KF, :], 0.0), CONSTANTS_SET)

            def deviations(b, g):
                t = g % NG * 4
                pool.wait_ge(mean_done, b * (2 * NG) + g + 1)
                pool.tensor_tensor(rstd[:, t:t + 4], mv[:, t:t + 4, 1], epsilon[:, :], ALU.add).then_inc(eps_done, 1)
                pool.wait_ge(eps_done, b * (2 * NG) + g + 1)
                pool.tensor_tensor(rstd[:, t:t + 4], rstd[:, t:t + 4], minus_half[:, :], ALU.pow).then_inc(rstd_done, 1)

            for g in range(NG):
                deviations(0, g)

            def row(b, more):
                pool.wait_ge(rstd_done, b * (2 * NG) + NG)
                pool.wait_ge(split_mm, b * SPLITS + S_ATT)
                passed(pool)
                pool.memset(qkv_head[:, :, :, HC:HC + 1], QSCALE).then_inc(ones_set, 1)
                pool.wait_ge(ones_set, b + 1)
                for g in range(NG):
                    deviations(b, NG + g)
                if more:
                    for g in range(NG):
                        deviations(b + 1, g)

            with pool.Fori(0, B - 1) as b:
                row(b, True)
            row(B - 1, False)

        @block.scalar
        def _(act):
            act.wait_ge(cond_in_s, 16)
            act.activation(silu_c, cond_in, ACT.Silu).then_inc(silu_done, 1)
            for j, (src, h, l, n, last) in enumerate(jobs):
                act.wait_ge(w_in[j % STAGES], 32 * (j // STAGES + 1))
                if j < W1_JOB:
                    h, stage = of_head(h), by_head(stage_of(j))
                    for k in range(3):
                        last_write = act.activation(h[:, k], stage[:, k], ACT.Copy, scale=WSCALE)
                    last_write.then_inc(w_high, 1)
                else:
                    act.activation(h, stage_of(j), ACT.Copy, scale=WSCALE).then_inc(w_high, 1)

            def high_parts(b, jobs):
                for j in jobs:
                    c, bank, at, vectors = split_place(b, j)
                    act.wait_ge(split_mm, b * SPLITS + j + 1)
                    for r, dst in [(slice(0, P), xh[:, c, at])] + [(slice(0, REM), xb[0:REM, at])] * (c == KF and j < S_LN2):
                        if vectors:
                            last = act.activation(dst, ps[r, bank, :], ACT.Identity, bias=vectors[0][r], scale=vectors[1][r])
                        else:
                            last = act.activation(dst, ps[r, bank, :], ACT.Copy)
                    last.then_inc(high_done, 1)

            act.wait_ge(mod_cp, 1)
            high_parts(0, range(KC))

            def row(b, more):
                high_parts(b, range(KC, S_ATT))
                act.wait_ge(stored, b * (NB * E * 16))
                passed(act)
                with act.Fori(0, NT // 2) as i:
                    for u in range(2):
                        for k in range(2):
                            act.wait_ge(qkv_mm[k], b * NT + i * 2 + (u + 1))
                            if k == 0:
                                act.wait_ge(qkv_stored[u], b * (NT // 2 * 16) + i * 16)
                            for bank in (2 * k, 2 * k + 1):
                                h, qkv = in_bank(u, bank)
                                dst = qkv_tok[:, u, h, :]
                                for part, at in enumerate((QL + DH, KH)):
                                    act.activation(dst[:, :, at:at + 2 * DH].rearrange("p h (r d) -> p h r d", r=2),
                                                   qkv[:, :, part].unsqueeze(2).broadcast_to([P, 4, 2, DH]),
                                                   ACT.Copy, scale=QSCALE / WSCALE)
                                last = act.activation(dst[:, :, VH:VH + DH], qkv[:, :, 2], ACT.Copy, scale=QSCALE / WSCALE)
                            last.then_inc(qkv_high, 1)

                def attend(i, n, live):
                    G = b * GROUPS + i
                    if live(0):
                        act.wait_ge(qk_turned, G + 1)
                        act.wait_ge(scores_mm, before(b, GROUPS, i, 2))
                        act.activation(qk_t[0:3 * DH, n % 2, :, :].rearrange("p k t -> p (k t)"), ps_half[0:3 * DH, n % 2, :],
                                       ACT.Copy).then_inc(qk_copied, 1)
                    if live(2):
                        act.wait_ge(probs_turned, G - 1)
                        act.wait_ge(out_mm, before(b, GROUPS, i - 2, 4))
                        act.activation(probs_h[:, (n - 2) % 4, :], ps[:, 4 + n % 2, :], ACT.Copy).then_inc(probs_high, 1)
                    if live(1):
                        act.wait_ge(shifted, G)
                        act.activation(probs[:, (n - 1) % 2, :], probs[:, (n - 1) % 2, :], ACT.Exp,
                                       scale=SCALE / QSCALE ** 2).then_inc(exp_done, 1)

                pipeline(act, attend)

                high_parts(b, range(S_ATT, S_LN2 + KC))

                def mlp_block(q, extra):
                    for m in range(MF):
                        act.wait_ge(fc1_mm, b * (NB * MF) + q * MF + (m + 1))
                        act.wait_ge(g_low, b * (NB * MF) + q * MF + max(0, m - 2))
                        act.activation(gelu[m % 3], ps[:, fc1_bank(m), 0:MB], ACT.Gelu, bias=f_bias[:, m:m + 1],
                                       scale=1 / WSCALE).then_inc(gelu_done, 1)
                        extra(m)

                def late(m):
                    c = m - LATE_AT
                    if 0 <= c < KC:
                        high_parts(b, range(S_LN2 + KC + c, S_LN2 + KC + c + 1))

                def next_row(m):
                    c = m - NEXT_AT
                    if c == 0:
                        act.wait_ge(mod_cp, b + 2)
                    if 0 <= c < KC:
                        high_parts(b + 1, range(c, c + 1))

                mlp_block(0, late)
                with act.Fori(1, NB - 1) as q:
                    mlp_block(q, lambda m: None)
                mlp_block(NB - 1, next_row if more else lambda m: None)

            with act.Fori(0, B - 1) as b:
                row(b, True)
            row(B - 1, False)

        @block.vector
        def _(dve):
            dve.wait_ge(silu_tr, 1)
            dve.tensor_copy(silu_t[:, 0:KF, :], ps[:, 7, 0:KF * B].rearrange("p (k b) -> p k b", b=B)).then_inc(silu_cp, 1)
            dve.tensor_copy(silu_t[0:REM, KF, :], ps[0:REM, 7, KF * B:KC * B]).then_inc(silu_cp, 1)
            dve.wait_ge(cols_tr, 1)
            dve.tensor_copy(f_bias[:, :], ps[:, 7, 64:64 + MF]).then_inc(cols_cp, 1)
            dve.wait_ge(rows_loaded, 16 * 6)
            dve.tensor_scalar(bias_h, bias_f, WSCALE, None, ALU.mult).then_inc(bias_split, 1)
            dve.wait_ge(bias_split, 1)
            dve.scalar_tensor_tensor(out=bias_l, in0=bias_f, scalar=WSCALE, in1=bias_h, op0=ALU.mult, op1=ALU.subtract).then_inc(bias_split, 1)
            dve.wait_ge(ada_mm, KC)
            dve.wait_ge(ada_b_in, 16)
            full_banks = VECTORS * D // 512
            dve.tensor_tensor(ada_out[:, 0:full_banks * 512].rearrange("b (k n) -> b k n", n=512), ps[0:B, 0:full_banks, :],
                              ada_bias[:, 0:full_banks * 512].rearrange("b (k n) -> b k n", n=512), ALU.add)
            rest = VECTORS * D - full_banks * 512
            dve.tensor_tensor(ada_out[:, full_banks * 512:], ps[0:B, full_banks, 0:rest], ada_bias[:, full_banks * 512:], ALU.add).then_inc(ada_added, 1)
            dve.wait_ge(ada_added, 1)
            for v in (GATE_MSA, GATE_MLP):
                gate = ada_out[:, v * D:(v + 1) * D]
                dve.tensor_scalar(gate, gate, 1 / WSCALE, None, ALU.mult).then_inc(gates_scaled, 1)
            dve.wait_ge(mods_tr, 1)
            dve.tensor_copy(mods[:, :, :], ps[:, 7, 0:VECTORS * KC * B].rearrange("p (n b) -> p b n", b=B)).then_inc(mods_set, 1)
            dve.wait_ge(mods_set, 1)
            for v in (SCALE_MSA, SCALE_MLP):
                dve.tensor_scalar(mods[:, :, v * KC:(v + 1) * KC], mods[:, :, v * KC:(v + 1) * KC], 1.0, None, ALU.add).then_inc(mods_set, 1)
            for j, (src, h, l, n, last) in enumerate(jobs):
                dve.wait_ge(w_high, j + 1)
                r = slice(0, REM if last else P)
                if j < W1_JOB:
                    for k in range(3):
                        last_write = dve.scalar_tensor_tensor(out=of_head(l[r])[:, k], in0=by_head(stage_of(j)[r])[:, k], scalar=WSCALE,
                                                              in1=of_head(h[r])[:, k], op0=ALU.mult, op1=ALU.subtract)
                    last_write.then_inc(w_low, 1)
                else:
                    dve.scalar_tensor_tensor(out=l[r], in0=stage_of(j)[r], scalar=WSCALE, in1=h[r], op0=ALU.mult, op1=ALU.subtract).then_inc(w_low, 1)

            def statistics(t, src):
                for k in range(2):
                    last = dve.bn_stats(stats[:, t, k, :], src[:, t, k * HALF:(k + 1) * HALF])
                if t % 4 == 3:
                    last.then_inc(stats_done, 1)

            def means(b, g):
                dve.wait_ge(stats_done, b * (2 * NG) + g + 1)
                passed(dve)
                for t in range(g % NG * 4, g % NG * 4 + 4):
                    last = dve.bn_aggr(mv[:, t, :], stats[:, t, :, :])
                last.then_inc(mean_done, 1)

            def normalize(b, t, src, g):
                if t % 4 == 0:
                    dve.wait_ge(mean_done, b * (2 * NG) + g + 1)
                    dve.wait_ge(rstd_done, b * (2 * NG) + g + 1)
                last = dve.tensor_scalar(xn[:, t, :], src[:, t, :], mv[:, t, 0:1], rstd[:, t:t + 1], ALU.subtract, ALU.mult)
                if t % 4 == 3:
                    last.then_inc(norm_done, 1)

            def low_parts(b, jobs):
                def add_shift(j):
                    c, bank, at, vectors = split_place(b, j)
                    r, dst = (slice(0, P), xl) if c < KF else (slice(REM, P), xh)
                    dve.wait_ge(unshifted, b * UNSHIFTED + unshifted_before(j) + 1)
                    dve.tensor_scalar(dst[r, c, at], low32[j % 3][r], vectors[0][r], None, ALU.add).then_inc(low_done, 1)

                late = None
                for j in jobs:
                    c, bank, at, vectors = split_place(b, j)
                    r, dst = (slice(0, P), xl) if c < KF else (slice(REM, P), xh)
                    dve.wait_ge(high_done, b * SPLITS + j + 1)
                    if vectors:
                        if j >= 3:
                            dve.wait_ge(low_done, b * SPLITS + j - 2)
                        dve.scalar_tensor_tensor(out=low32[j % 3][r], in0=ps[r, bank, :], scalar=vectors[1][r], in1=xh[r, c, at],
                                                 op0=ALU.mult, op1=ALU.subtract).then_inc(unshifted, 1)
                        if late is not None:
                            add_shift(late)
                        late = j
                    else:
                        dve.tensor_tensor(dst[r, c, at], ps[r, bank, :], xh[r, c, at], ALU.subtract).then_inc(low_done, 1)
                if late is not None:
                    add_shift(late)

            def take_modulation(b):
                dve.wait_ge(low_done, b * SPLITS)
                dve.tensor_copy(mod[:, :, :], mods[:, b:b + 1, :] if isinstance(b, int) else mods[:, bass.ds(b, 1), :]).then_inc(mod_cp, 1)
                dve.wait_ge(mod_cp, b + 1)

            dve.wait_ge(x_in, E * 16)
            for t in range(NT):
                statistics(t, xn)
                if t % 4 == 3:
                    means(0, t // 4)
            for t in range(NT):
                normalize(0, t, xn, t // 4)
            dve.wait_ge(mods_set, 3)
            take_modulation(0)
            low_parts(0, range(KC))

            def row(b, more):
                dve.wait_ge(x2_done, b * NT)
                low_parts(b, range(KC, S_ATT))
                passed(dve)
                with dve.Fori(0, NT // 2) as i:
                    for u in range(2):
                        for k in range(2):
                            dve.wait_ge(qkv_high, b * (2 * NT) + i * 4 + (u * 2 + k + 1))
                            for bank in (2 * k, 2 * k + 1):
                                h, qkv = in_bank(u, bank)
                                dst = qkv_tok[:, u, h, :]
                                for part, (low, high) in enumerate(((QL, QL + DH), (KH + 2 * DH, KH), (VL, VH))):
                                    last = dve.scalar_tensor_tensor(out=dst[:, :, low:low + DH], in0=qkv[:, :, part], scalar=QSCALE / WSCALE,
                                                                    in1=dst[:, :, high:high + DH], op0=ALU.mult, op1=ALU.subtract)
                            last.then_inc(qkv_done, 1)

                def attend(i, n, live):
                    G = b * GROUPS + i
                    s1, s3, s4, s5 = (n - 1) % 2, (n - 3) % 2, n % 2, (n - 5) % 2
                    scores = ps[:, 2 + s1, :].rearrange("p (k c) -> p k c", k=4)
                    outputs = lambda s: ps[:, 6 + s, 0:4 * (DH + 1)].rearrange("p (k c) -> p k c", k=4)
                    if live(1):
                        dve.wait_ge(scores_mm, G)
                        dve.tensor_reduce(negmax[:, s1, :], scores, AX.X, ALU.max, negate=True).then_inc(max_done, 1)
                    if live(5):
                        dve.wait_ge(inv_done, G - 4)
                        if isinstance(i, int) and i == 5:
                            for u in range(2):
                                dve.wait_ge(qkv_stored[u], (b + 1) * (NT // 2 * 16))
                        dve.tensor_tensor(tok_f[:, bass.ds((i - 5) * (4 * DH), 4 * DH)].rearrange("p (k c) -> p k c", k=4),
                                          outputs(s5)[:, :, 0:DH], inv_sum[:, s5, :].unsqueeze(2).broadcast_to([P, 4, DH]), ALU.mult).then_inc(out_done, 1)
                    if live(1):
                        dve.wait_ge(max_done, G)
                        dve.wait_ge(probs_turned, before(b, GROUPS, i - 1, 2))
                        dve.tensor_tensor(probs[:, s1, :].rearrange("p (k c) -> p k c", k=4), scores,
                                          negmax[:, s1, :].unsqueeze(2).broadcast_to([P, 4, P]), ALU.add).then_inc(shifted, 1)
                    if live(3):
                        slot = (n - 3) % 4
                        dve.wait_ge(probs_high, G - 2)
                        dve.wait_ge(out_mm, before(b, GROUPS, i - 3, 4))
                        dve.tensor_tensor(probs_l[:, slot, :], ps[:, 4 + s3, :], probs_h[:, slot, :], ALU.subtract).then_inc(probs_low, 1)
                    if live(4):
                        dve.wait_ge(out_mm, G - 3)
                        dve.reciprocal(inv_sum[:, s4, :], outputs(s4)[:, :, DH]).then_inc(inv_done, 1)

                pipeline(dve, attend)

                low_parts(b, range(S_ATT, S_LN2))
                dve.wait_ge(xres_in, (b + 1) * (E * 16))
                dve.wait_ge(gates_in, (b + 1) * 32)
                for t in range(NT):
                    bank = proj_bank(t)
                    dve.wait_ge(proj_mm, b * NT + t + 1)
                    dve.tensor_tensor(tok[:, t, :].rearrange("p (k n) -> p k n", k=2), ps[:, bank:bank + 2, 0:HALF],
                                      gates[:, 0, :].rearrange("p (k n) -> p k n", k=2), ALU.mult).then_inc(proj_gated, 1)
                    dve.wait_ge(proj_gated, b * NT + t + 1)
                    dve.tensor_tensor(tok[:, t, :], tok[:, t, :], xn[:, t, :], ALU.add).then_inc(x1_done, 1)
                    dve.wait_ge(x1_done, b * NT + t + 1)
                    statistics(t, tok)
                    if t % 4 == 3:
                        means(b, NG + t // 4)
                    if t == 4:
                        for n in range(4):
                            normalize(b, n, tok, NG)
                    if t == 5:
                        low_parts(b, range(S_LN2, S_LN2 + KF))
                    if t == 6:
                        low_parts(b, range(S_LN2 + KF, S_LN2 + KC))

                def mlp_block(q, extra):
                    for m in range(MF):
                        M = b * (NB * MF) + q * MF + (m + 1)
                        dve.wait_ge(gelu_done, M)
                        dve.wait_ge(g_used, b * (NB * MF) + q * MF + max(0, m - 2))
                        dve.tensor_copy(gh[:, m % 3, :], gelu[m % 3]).then_inc(g_high, 1)
                        dve.wait_ge(g_high, M)
                        dve.tensor_tensor(gl[:, m % 3, :], gelu[m % 3], gh[:, m % 3, :], ALU.subtract).then_inc(g_low, 1)
                        extra(m)
                    if isinstance(q, int) and q == NB - 1 and more:
                        dve.wait_ge(low_done, (b + 1) * SPLITS + KC)
                    else:
                        dve.wait_ge(low_done, (b + 1) * SPLITS)
                    passed(dve)
                    for u in range(2):
                        t = q * 2 + u
                        tile = slice(t, t + 1) if isinstance(t, int) else bass.ds(t, 1)
                        dve.wait_ge(fc2_mm, b * NT + t + 1)
                        dve.tensor_tensor(gated[u].rearrange("p (k n) -> p k n", k=2), ps[:, 2 * u:2 * u + 2, 0:HALF],
                                          gates[:, 1, :].rearrange("p (k n) -> p k n", k=2), ALU.mult).then_inc(mlp_gated, 1)
                        dve.wait_ge(mlp_gated, b * NT + t + 1)
                        x2 = tok[:, tile, :].rearrange("p t d -> p (t d)")
                        dve.tensor_tensor(x2, x2, gated[u], ALU.add).then_inc(x2_done, 1)

                def late(m):
                    if m < 2:
                        for n in (4 + 2 * m, 5 + 2 * m):
                            normalize(b, n, tok, NG + 1)
                    c = m - LATE_AT
                    if 0 <= c < KC:
                        low_parts(b, range(S_LN2 + KC + c, S_LN2 + KC + c + 1))

                def next_row(m):
                    if m == 0:
                        dve.wait_ge(x_in, (b + 2) * (E * 16))
                        passed(dve)
                    if m < NT // 2:
                        for t in (2 * m, 2 * m + 1):
                            statistics(t, xn)
                        if m % 2:
                            means(b + 1, m // 2)
                    for t in {4: (0, 1), 5: (2, 3), 7: (4, 5), 8: (6, 7)}.get(m, ()):
                        normalize(b + 1, t, xn, t // 4)
                    c = m - NEXT_AT
                    if 0 <= c < KC:
                        if c == 0:
                            dve.wait_ge(x2_done, b * NT + NT - 2)
                            take_modulation(b + 1)
                        low_parts(b + 1, range(c, c + 1))

                mlp_block(0, late)
                with dve.Fori(1, NB - 1) as q:
                    mlp_block(q, lambda m: None)
                mlp_block(NB - 1, next_row if more else lambda m: None)

            with dve.Fori(0, B - 1) as b:
                row(b, True)
            row(B - 1, False)

        @block.tensor
        def _(pe):
            pe.wait_ge(silu_done, 1)
            pe.wait_ge(consts_set, IDENT_SET)
            for k in range(KC):
                n = min(P, D - k * P)
                last = pe.transpose(ps[0:n, 7, k * B:(k + 1) * B], silu_c[:, k * P:k * P + n], ident[0:B, 0:B])
            last.then_inc(silu_tr, 1)
            pe.wait_ge(silu_cp, 2)
            pe.wait_ge(rows_loaded, 16 * 6)
            pe.transpose(ps[:, 7, 64:64 + MF], col_rows, ident[0:MF, 0:MF]).then_inc(cols_tr, 1)
            for k in range(KC):
                rows = min(P, D - k * P)
                pe.wait_ge(ada_w_in[k % 3], 16 * (k // 3 + 1))
                for n in range(0, VECTORS * D, 512):
                    w = min(512, VECTORS * D - n)
                    last = pe.matmul(ps[0:B, n // 512, 0:w], silu_t[0:rows, k, :], ada_stage[k % 3][0:rows, n:n + w],
                                     start=(k == 0), stop=(k == KC - 1))
                last.then_inc(ada_mm, 1)
            pe.wait_ge(cols_cp, 1)
            pe.wait_ge(gates_scaled, 2)
            for v in range(VECTORS):
                for c in range(KC):
                    at = (v * KC + c) * B
                    if c < KF:
                        pe.transpose(ps[:, 7, at:at + B], ada_out[:, v * D + c * P:v * D + (c + 1) * P], ident[0:B, 0:B])
                    else:
                        pe.transpose(ps[:, 7, at:at + B], ada_out[:, (v + 1) * D - P:(v + 1) * D], ident[0:B, 0:B])
                        last = pe.transpose(ps[0:REM, 7, at:at + B], ada_out[:, (v + 1) * D - REM:(v + 1) * D], ident[0:B, 0:B])
            last.then_inc(mods_tr, 1)
            pe.wait_ge(mods_set, 1)
            pe.wait_ge(w_low, len(jobs))
            pe.wait_ge(bias_in, 16 * 6)
            pe.wait_ge(consts_set, CONSTANTS_SET)

            def passes(wh, wl, biased=False):
                for c in range(KC):
                    yield xh[:, c, :], wh[:, c, :]
                for c in range(KF):
                    yield xh[:, c, :], wl[:, c, :]
                yield xb[:, :] if biased else xh[:, KF, :], wl[:, KF, :]
                for c in range(KF):
                    yield xl[:, c, :], wh[:, c, :]

            def tokens(t):
                return slice(t * P, (t + 1) * P) if isinstance(t, int) else bass.ds(t * P, P)

            def by_tokens(t, bank, wh, wl, col, n, done):
                ops = list(passes(wh, wl, biased=True))
                for i, (xa, wa) in enumerate(ops):
                    for k in range(2):
                        last = pe.matmul(ps[:, bank + k, 0:n], xa[:, tokens(t)], wa[:, col + k * n:col + (k + 1) * n],
                                         start=(i == 0), stop=(i == len(ops) - 1))
                last.then_inc(done, 1)

            def turn(b, j0, src, chunks=range(KC)):
                t0 = j0 // KC % NG * 4
                for j in (j0 + c for c in chunks):
                    c, bank, _, _ = split_place(b, j)
                    if j < S_LN1 + KC or j >= S_LN2 + KC:
                        if not isinstance(b, int) or b:
                            pe.wait_ge(low_done, b * SPLITS + j)
                    elif j < S_ATT:
                        if c % 4 == 0:
                            pe.wait_ge(low_done, b * SPLITS + (j if c == 0 else j - 3))
                    elif t0:
                        pe.wait_ge(low_done, b * SPLITS + j - KC + 1)
                    elif j == S_LN2 + KF:
                        pe.wait_ge(low_done, b * SPLITS + S_LN2 + 1)
                    for t in range(4):
                        at = slice(t * P, (t + 1) * P)
                        if c < KF:
                            last = pe.transpose(ps[:, bank, at], src[:, t0 + t, c * P:(c + 1) * P], ident[:, :])
                        else:
                            pe.transpose(ps[:, bank, at], src[:, t0 + t, D - P:D], ident[:, :])
                            last = pe.transpose(ps[0:REM, bank, at], src[:, t0 + t, KF * P:D], ident[:, :])
                    last.then_inc(split_mm, 1)

            pe.wait_ge(norm_done, 1)
            turn(0, S_LN1, xn)

            def row(b, more):
                pe.wait_ge(norm_done, b * (2 * NG) + 2)
                passed(pe)
                turn(b, S_LN1 + KC, xn, range(KF))

                pe.wait_ge(mlp_gated, b * NT)
                pe.wait_ge(low_done, b * SPLITS + KC)
                by_tokens(0, 0, wq_h, wq_l, 0, QC, qkv_mm[0])
                turn(b, S_LN1 + KC, xn, range(KF, KC))
                by_tokens(0, 2, wq_h, wq_l, 2 * QC, QC, qkv_mm[1])
                pe.wait_ge(low_done, b * SPLITS + S_ATT)
                for k in range(2):
                    by_tokens(1, 4 + 2 * k, wq_h, wq_l, k * 2 * QC, QC, qkv_mm[k])
                with pe.Fori(1, NT // 2) as i:
                    for u in range(2):
                        for k in range(2):
                            pe.wait_ge(qkv_done, b * (2 * NT) + i * 4 + (2 * u + k - 3))
                            by_tokens(i * 2 + u, 4 * u + 2 * k, wq_h, wq_l, k * 2 * QC, QC, qkv_mm[k])
                pe.wait_ge(qkv_done, (b + 1) * (2 * NT) - 2)
                pe.wait_ge(ones_set, b + 1)
                passed(pe)

                def attend(i, n, live):
                    G = b * GROUPS + i
                    if live(0):
                        pe.wait_ge(heads_in[n // 2], b * (GROUPS // RING * 16) + (i - n) * 2 + 16)
                        pe.wait_ge(qk_copied, before(b, GROUPS, i, 2))
                        passed(pe)
                        for half, at in enumerate((QL, KH)):
                            for k in range(4):
                                last = pe.transpose(ps_half[0:3 * DH, n % 2, (half * 4 + k) * P:(half * 4 + k + 1) * P],
                                                    qkv_head[:, n, k, at:at + 3 * DH], ident_h[:, :])
                        last.then_inc(qk_turned, 1)
                    if live(1):
                        s = (n - 1) % 2
                        pe.wait_ge(qk_copied, G)
                        pe.wait_ge(shifted, before(b, GROUPS, i - 1, 2))
                        pe.matmul(ps[:, 2 + s, :].rearrange("p (k c) -> p k c", k=4), own[:, :],
                                  others[:, :].unsqueeze(1).broadcast_to([P, 4, P]), start=True, stop=False)
                        for k in range(4):
                            last = pe.matmul(ps[:, 2 + s, k * P:(k + 1) * P], qk_t[0:3 * DH, s, 0, k * P:(k + 1) * P],
                                             qk_t[0:3 * DH, s, 1, k * P:(k + 1) * P], start=False, stop=(k == 3))
                        last.then_inc(scores_mm, 1)
                    if live(4):
                        s = n % 2
                        pe.wait_ge(probs_low, G - 3)
                        pe.wait_ge(out_done, before(b, GROUPS, i - 4, 2))
                        for k in range(4):
                            at, o = slice(k * P, (k + 1) * P), k * (DH + 1)
                            v = qkv_head[:, (n - 4) % RING, k, :]
                            pe.matmul(ps[:, 6 + s, o:o + DH + 1], probs_h[:, n % 4, at], v[:, VH:VH + DH + 1], start=True, stop=False)
                            pe.matmul(ps[:, 6 + s, o:o + DH], probs_h[:, n % 4, at], v[:, VL:VL + DH], start=False, stop=False)
                            last = pe.matmul(ps[:, 6 + s, o:o + DH + 1], probs_l[:, n % 4, at], v[:, VH:VH + DH + 1], start=False, stop=True)
                        last.then_inc(out_mm, 1)
                    if live(2):
                        s = n % 2
                        pe.wait_ge(exp_done, G - 1)
                        if isinstance(i, int) and i == 2:
                            pe.wait_ge(qkv_done, (b + 1) * (2 * NT))
                        pe.wait_ge(probs_low, before(b, GROUPS, i - 2, 2))
                        for k in range(4):
                            last = pe.transpose(ps[:, 4 + s, k * P:(k + 1) * P], probs[:, s, k * P:(k + 1) * P], ident[:, :])
                        last.then_inc(probs_turned, 1)
                    if isinstance(i, int) and i == GROUPS + 1:
                        pe.wait_ge(qk_copied, (b + 1) * GROUPS)
                        pe.wait_ge(shifted, (b + 1) * GROUPS)
                        pe.wait_ge(out_done, b * GROUPS + GROUPS // 2)
                        turn(b, S_ATT, tok, range(KF))

                pipeline(pe, attend)

                pe.wait_ge(out_done, (b + 1) * GROUPS)
                turn(b, S_ATT, tok, range(KF, KC))
                turn(b, S_ATT + KC, tok)
                pe.wait_ge(low_done, b * SPLITS + S_ATT + KC)
                by_tokens(0, proj_bank(0), wp_h, wp_l, 0, HALF, proj_mm)
                pe.wait_ge(low_done, b * SPLITS + S_LN2)
                by_tokens(1, proj_bank(1), wp_h, wp_l, 0, HALF, proj_mm)
                with pe.Fori(1, NT // 2 - 1) as i:
                    for u in range(2):
                        pe.wait_ge(proj_gated, b * NT + i * 2 + (u - 1))
                        by_tokens(i * 2 + u, proj_bank(u), wp_h, wp_l, 0, HALF, proj_mm)
                pe.wait_ge(norm_done, b * (2 * NG) + NG + 1)
                passed(pe)
                turn(b, S_LN2, xn, range(KF))
                for t in (NT - 2, NT - 1):
                    if t == NT - 1:
                        turn(b, S_LN2, xn, range(KF, KC))
                    pe.wait_ge(proj_gated, b * NT + t - 1)
                    by_tokens(t, proj_bank(t), wp_h, wp_l, 0, HALF, proj_mm)
                pe.wait_ge(proj_gated, (b + 1) * NT - 1)

                def turn_late(step):
                    c = step - LATE_AT
                    if 0 <= c < KC:
                        if c == 0:
                            pe.wait_ge(norm_done, b * (2 * NG) + NG + 2)
                            passed(pe)
                        turn(b, S_LN2 + KC, xn, range(c, c + 1))

                def turn_next(step):
                    c = step - NEXT_AT
                    if 0 <= c < KC:
                        if c == 0:
                            pe.wait_ge(norm_done, (b + 1) * (2 * NG) + 1)
                            passed(pe)
                        turn(b + 1, S_LN1, xn, range(c, c + 1))

                def mlp_block(q, between):
                    for step in range(MF + 2):
                        if step < MF:
                            m = step
                            pe.wait_ge(gelu_done, b * (NB * MF) + q * MF + max(0, m - 2))
                            if isinstance(q, int) and q == 0 and m == 2:
                                pe.wait_ge(proj_gated, (b + 1) * NT)
                            if m == 0:
                                pe.wait_ge(low_done, (b + 1) * SPLITS - (KC if isinstance(q, int) and q == 0 else 0))
                            ops = list(passes(w1_h, w1_l))
                            for i, (xa, wa) in enumerate(ops):
                                last = pe.matmul(ps[:, fc1_bank(m), 0:MB], wa[:, m * P:(m + 1) * P], xa[:, bass.ds(q * MB, MB)],
                                                 start=(i == 0), stop=(i == len(ops) - 1))
                            last.then_inc(fc1_mm, 1)
                        between(step)
                        if step >= 2:
                            m = step - 2
                            if m == 0:
                                pe.wait_ge(mlp_gated, b * NT + q * 2)
                            pe.wait_ge(g_low, b * (NB * MF) + q * MF + (m + 1))
                            for u in range(2):
                                for i, (ga, wa) in enumerate(((gh, w2_h), (gh, w2_l), (gl, w2_h))):
                                    for k in range(2):
                                        last = pe.matmul(ps[:, 2 * u + k, 0:HALF], ga[:, m % 3, u * P:(u + 1) * P],
                                                         wa[:, m, k * HALF:(k + 1) * HALF], start=(m == 0 and i == 0), stop=False)
                            last.then_inc(g_used, 1)
                    for u in range(2):
                        for k in range(2):
                            last = pe.matmul(ps[:, 2 * u + k, 0:HALF], pick[:, :], bias_rows[:, k * HALF:(k + 1) * HALF],
                                             start=False, stop=True)
                        last.then_inc(fc2_mm, 1)

                mlp_block(0, turn_late)
                with pe.Fori(1, NB - 1) as q:
                    mlp_block(q, lambda step: None)
                mlp_block(NB - 1, turn_next if more else lambda step: None)

            with pe.Fori(0, B - 1) as b:
                row(b, True)
            row(B - 1, False)


_INS = ['x', 'cond_1152', 'L0_cond_qkv_w', 'L0_cond_qkv_b', 'L0_cond_proj_w', 'L0_cond_proj_b', 'L0_cond_fc1_w',
        'L0_cond_fc1_b', 'L0_cond_fc2_w', 'L0_cond_fc2_b', 'L0_cond_ada_w', 'L0_cond_ada_b']
_OUTS = [((8, 1024, 576), 'float32')]


def kernel(**inputs):
    import numpy as _np
    import concourse.bacc as _bacc
    from concourse import mybir as _mybir
    from concourse.bass_utils import run_bass_kernel_spmd as _run

    nc = _bacc.Bacc("TRN2", target_bir_lowering=False, num_devices=1)
    arrays, args = {}, []
    for name in _INS:
        a = _np.ascontiguousarray(inputs[name])
        arrays[f"in_{name}_dram"] = a
        args.append(nc.dram_tensor(f"in_{name}_dram", a.shape, _mybir.dt.from_np(a.dtype), kind="ExternalInput").ap())
    for i, (shape, dtype) in enumerate(_OUTS):
        dt = _mybir.dt.from_np(_np.dtype(dtype))
        args.append(nc.dram_tensor(f"out_{i}_dram", shape, dt, kind="ExternalOutput").ap())
    block_kernel(nc, *args)
    r = _run(nc, [arrays], core_ids=[0])
    got = tuple(r.results[0][f"out_{i}_dram"] for i in range(len(_OUTS)))
    return got[0]
```
